# Optimizing a Trainium2 kernel written in Bass

```python
import numpy as np
import jax
import jax.numpy as jnp

def _softmax(x, axis=-1):
    return jax.nn.softmax(x, axis=axis)

def _gelu(x):
    return jax.nn.gelu(x, approximate=True)

def _silu(x):
    return jax.nn.silu(x)

def _sigmoid(x):
    return jax.nn.sigmoid(x)

def _layernorm(x, axis=-1, eps=1e-05):
    m = jnp.mean(x, axis=axis, keepdims=True)
    v = jnp.var(x, axis=axis, keepdims=True)
    return (x - m) / jnp.sqrt(v + eps)

def _scatter_add(tgt, idx, src, axis=0):
    return tgt.at[idx].add(src)

def _segment_sum(src, seg, n):
    return jax.ops.segment_sum(src, seg, n)
kernel_name = 'mk_adaln_d1_jaxref_r4_289a54'

def setup_inputs(seed: int=0):
    np.random.seed(seed)
    _w = jnp.asarray

    def _L0_attn_setup():
        import jax, jax.numpy as jnp
        import numpy as np
        HID = 512
        HEADS = 16
        HD = HID // HEADS
        EPS = 1e-06

        def _heads(x, b, s):
            return x.reshape(b, s, HEADS, HD).transpose(0, 2, 1, 3)
        key = jax.random.key(seed)
        ks = jax.random.split(key, 9)
        s = 1.0 / np.sqrt(HID)
        return {'hidden_states': jax.random.normal(ks[0], (4, 1024, HID), jnp.float32), 'q_w': jax.random.normal(ks[1], (HID, HID), jnp.float32) * s, 'q_b': jnp.zeros((HID,), jnp.float32), 'k_w': jax.random.normal(ks[2], (HID, HID), jnp.float32) * s, 'k_b': jnp.zeros((HID,), jnp.float32), 'v_w': jax.random.normal(ks[3], (HID, HID), jnp.float32) * s, 'v_b': jnp.zeros((HID,), jnp.float32), 'o_w': jax.random.normal(ks[4], (HID, HID), jnp.float32) * s, 'o_b': jnp.zeros((HID,), jnp.float32)}
    _L0_attn_in = _L0_attn_setup()

    def _L0_ffn_setup():
        import jax, jax.numpy as jnp
        import numpy as np
        HIDDEN = 512
        INTER = 1376
        LUT_SIZE = 16

        def _ghost_linear(x, idx, lut):
            w = lut[idx]
            return jnp.einsum('bsh,oh->bso', x, w)
        key = jax.random.key(seed)
        k_x, k_lut, k_g, k_u, k_d = jax.random.split(key, 5)
        x = jax.random.normal(k_x, (2, 1024, HIDDEN), dtype=jnp.float32)
        lut = jax.random.normal(k_lut, (LUT_SIZE,), dtype=jnp.float32) * 0.02
        gate_idx = jax.random.randint(k_g, (INTER, HIDDEN), 0, LUT_SIZE, dtype=jnp.int32)
        up_idx = jax.random.randint(k_u, (INTER, HIDDEN), 0, LUT_SIZE, dtype=jnp.int32)
        down_idx = jax.random.randint(k_d, (HIDDEN, INTER), 0, LUT_SIZE, dtype=jnp.int32)
        return {'x': x, 'lut': lut, 'gate_idx': gate_idx, 'up_idx': up_idx, 'down_idx': down_idx}
    _L0_ffn_in = _L0_ffn_setup()
    _L0_c = _w((lambda *s: np.random.randn(*s).astype(np.float32) * 0.05)(2, 512))
    _L0_wmod = _w((lambda *s: np.random.randn(*s).astype(np.float32) * 0.05)(512, 6 * 512) * 512 ** (-0.5))
    _d = {'L0_attn_hidden_states': _L0_attn_in['hidden_states'], 'L0_attn_q_w': _L0_attn_in['q_w'], 'L0_attn_q_b': _L0_attn_in['q_b'], 'L0_attn_k_w': _L0_attn_in['k_w'], 'L0_attn_k_b': _L0_attn_in['k_b'], 'L0_attn_v_w': _L0_attn_in['v_w'], 'L0_attn_v_b': _L0_attn_in['v_b'], 'L0_attn_o_w': _L0_attn_in['o_w'], 'L0_attn_o_b': _L0_attn_in['o_b'], 'L0_ffn_lut': _L0_ffn_in['lut'], 'L0_ffn_gate_idx': _L0_ffn_in['gate_idx'], 'L0_ffn_up_idx': _L0_ffn_in['up_idx'], 'L0_ffn_down_idx': _L0_ffn_in['down_idx'], 'L0_c': _L0_c, 'L0_wmod': _L0_wmod}
    _x0 = _d['L0_attn_hidden_states']
    _d['L0_attn_hidden_states'] = jax.random.normal(jax.random.fold_in(jax.random.key(seed), 1), (2, 2048, 512), dtype=_x0.dtype)
    del _x0
    return _d

def reference(L0_attn_hidden_states, L0_attn_q_w, L0_attn_q_b, L0_attn_k_w, L0_attn_k_b, L0_attn_v_w, L0_attn_v_b, L0_attn_o_w, L0_attn_o_b, L0_ffn_lut, L0_ffn_gate_idx, L0_ffn_up_idx, L0_ffn_down_idx, L0_c, L0_wmod):

    def _L0_attn_ref(hidden_states, q_w, q_b, k_w, k_b, v_w, v_b, o_w, o_b):
        import jax, jax.numpy as jnp
        import numpy as np
        HID = 512
        HEADS = 16
        HD = HID // HEADS
        EPS = 1e-06

        def _heads(x, b, s):
            return x.reshape(b, s, HEADS, HD).transpose(0, 2, 1, 3)
        b, s, _ = hidden_states.shape
        q = _heads(hidden_states @ q_w.T + q_b, b, s)
        k = _heads(hidden_states @ k_w.T + k_b, b, s)
        v = _heads(hidden_states @ v_w.T + v_b, b, s)
        qp = jax.nn.elu(q) + 1.0
        kp = jax.nn.elu(k) + 1.0
        kv = jnp.einsum('bhsd,bhse->bhde', kp, v)
        z = jnp.einsum('bhsd,bhd->bhs', qp, kp.sum(axis=2))[..., None]
        attn = jnp.einsum('bhsd,bhde->bhse', qp, kv) / (z + EPS)
        out = attn.transpose(0, 2, 1, 3).reshape(b, s, HID)
        return out @ o_w.T + o_b

    def _L0_ffn_ref(x, lut, gate_idx, up_idx, down_idx):
        import jax, jax.numpy as jnp
        import numpy as np
        HIDDEN = 512
        INTER = 1376
        LUT_SIZE = 16

        def _ghost_linear(x, idx, lut):
            w = lut[idx]
            return jnp.einsum('bsh,oh->bso', x, w)
        gate = _ghost_linear(x, gate_idx, lut)
        up = _ghost_linear(x, up_idx, lut)
        h = jax.nn.silu(gate) * up
        return _ghost_linear(h, down_idx, lut)
    x = L0_attn_hidden_states
    mod = (_silu(L0_c) @ L0_wmod).reshape(L0_c.shape[0], 6, 1, -1)
    sa, ca, ga, sb, cb, gb = (mod[:, 0], mod[:, 1], mod[:, 2], mod[:, 3], mod[:, 4], mod[:, 5])
    ga = (2 * (ga >= 0) - 1) * jnp.maximum(jnp.abs(ga), 0.25)
    gb = (2 * (gb >= 0) - 1) * jnp.maximum(jnp.abs(gb), 0.25)
    h = _layernorm(x, axis=-1) * (1 + ca) + sa
    x = x + ga * _L0_attn_ref(h, L0_attn_q_w, L0_attn_q_b, L0_attn_k_w, L0_attn_k_b, L0_attn_v_w, L0_attn_v_b, L0_attn_o_w, L0_attn_o_b)
    h = _layernorm(x, axis=-1) * (1 + cb) + sb
    x = x + gb * _L0_ffn_ref(h, L0_ffn_lut, L0_ffn_gate_idx, L0_ffn_up_idx, L0_ffn_down_idx)
    return x

_drawn_inputs = setup_inputs


def setup_inputs(seed=0):
    import zlib

    import numpy as np

    out = dict(_drawn_inputs(seed))
    spreads = {'L0_attn_q_b': (0.0, 0.8),
     'L0_attn_k_b': (0.0, 0.8),
     'L0_attn_v_b': (0.0, 0.329),
     'L0_attn_o_b': (0.0, 0.312)}
    factors = {'L0_attn_q_w': 8.0, 'L0_attn_k_w': 8.0, 'L0_attn_v_w': 8.0}
    for name, (base, spread) in spreads.items():
        noise = np.random.default_rng([zlib.crc32(name.encode()), seed]).standard_normal(out[name].shape)
        drawn = base * np.exp(spread * noise) if base else spread * noise
        out[name] = jnp.asarray(drawn.astype(out[name].dtype))
    for name, factor in factors.items():
        out[name] = (out[name] * factor).astype(out[name].dtype)
    return out
```

```python
from contextlib import ExitStack

import concourse.bass as bass
from concourse import mybir

ALU = mybir.AluOpType
ACT = mybir.ActivationFunctionType
AX = mybir.AxisListType
F32 = mybir.dt.float32
F16 = mybir.dt.float16
U32 = mybir.dt.uint32
I32 = mybir.dt.int32
RMAX = bass.bass_isa.ReduceOp.max

P = 128
BATCHES, SEQ, HID = 2, 2048, 512
HEADS = 16
HEAD = HID // HEADS
INTER = 1376
TABLE = 16
KC = HID // P
GROUP = 512
TILES = GROUP // P
GROUPS = BATCHES * SEQ // GROUP
PER_BATCH = SEQ // GROUP
FC = -(-INTER // P)
TAIL = INTER - (FC - 1) * P
OUTS = 2 * TILES + KC
LN_EPS = 1e-5
ATTN_EPS = 1e-6
EXPONENT, MAGNITUDE = 0x7F800000, 0x7FFFFFFF

GU_COLS = KC * 2 * INTER // GROUPS
DN_COLS = FC * HID // GROUPS
PIECE = max(GU_COLS // 2, DN_COLS)

(C_MAX, C_AMAX, C_POW, C_INV, C_SPLIT) = (0, 8, 16, 24, 32)
(S_K, S_V, S_Q, S_H1, S_H2, S_LUT, S_M0, S_M1) = range(8)
(C_INV_K, C_INV_V, C_INV_Q, C_INV_G, C_HID, C_INV_D, C_INV_O, C_TMP, C_NEG_Q) = (40, 41, 42, 43, 44, 45, 46, 48, 50)

FREE_GROUP = 1


def adaln_kernel(nc, x, qwT, qb, kwT, kb, vwT, vb, owT, ob, lut, gateT, upT, downT, cT, wmod, out):
    with ExitStack() as ctx:
        def sb(name, shape, dt):
            return ctx.enter_context(nc.sbuf_tensor(name, shape, dt))

        def sem(name):
            return ctx.enter_context(nc.semaphore(name))

        def part(arena, start, dt, *dims):
            n = 1
            for d in dims:
                n *= d
            words = n * (2 if dt == F16 else 4) // 4
            v = arena[:, start:start + words]
            if dt != U32:
                v = v.bitcast(dt)
            if len(dims) == 2:
                v = v.rearrange("p (a b) -> p a b", a=dims[0])
            elif len(dims) == 3:
                v = v.rearrange("p (a b c) -> p a b c", a=dims[0], b=dims[1])
            elif len(dims) == 4:
                v = v.rearrange("p (a b c d) -> p a b c d", a=dims[0], b=dims[1], c=dims[2])
            return v

        tile_w = KC * GROUP
        w_proj = sb("w_proj", [P, 3 * tile_w], U32)
        w_gu = sb("w_gu", [P, KC * 2 * INTER], U32)
        w_dn = sb("w_dn", [P, FC * HID], U32)
        work = sb("work", [P, 9 * PIECE], U32)
        whi = part(w_proj, 0, F16, 3, KC, HID)
        wlo = part(w_proj, 3 * tile_w // 2, F16, 3, KC, HID)
        mhi = part(w_proj, 0, F16, BATCHES, KC, HID)
        mlo = part(w_proj, tile_w, F16, BATCHES, KC, HID)
        mfull = part(w_proj, 2 * tile_w, F32, KC, HID)
        xn2 = part(w_proj, 2 * tile_w, F32, TILES, HID)
        gu = w_gu[:, :].bitcast(F16).rearrange("p (k w f h) -> p k w f h", k=KC, w=2, h=2)
        dn = w_dn[:, :].bitcast(F16).rearrange("p (j n h) -> p j n h", j=FC, h=2)
        raw = [part(w_gu, i * tile_w, F32, KC, HID) for i in range(2)] + [part(w_dn, 0, F32, KC, HID)]
        mod_at = {1: (w_gu, 2), 0: (w_gu, 3), 2: (w_gu, 4), 5: (work, 0), 4: (work, 1), 3: (w_dn, 1)}
        mod_raw = {s: part(a, i * tile_w, F32, KC, HID) for s, (a, i) in mod_at.items()}
        owt = part(work, 0, F32, KC, HID)
        att = part(work, tile_w, F32, KC, P)
        att_T = part(work, tile_w + HID, F32, KC, P)
        lk = [part(work, i * PIECE, U32, PIECE) for i in range(9)]
        qn_hi = part(work, 0, F16, KC, GROUP)
        qn_lo = part(work, tile_w // 2, F16, KC, GROUP)
        silu_g = part(work, tile_w, F32, 2, GROUP)
        hid_f = part(work, tile_w + 2 * GROUP, F32, 2, GROUP)
        hid_hi = part(work, tile_w + 4 * GROUP, F16, 2, GROUP)
        hid_lo = part(work, tile_w + 5 * GROUP, F16, 2, GROUP)

        xg = sb("xg", [P, 2, TILES, HID], F32)
        h_hi = sb("h_hi", [P, 2, KC, GROUP], F16)
        h_lo = sb("h_lo", [P, 2, KC, GROUP], F16)
        h_f = sb("h_f", [P, 2, GROUP], F32)
        qp = sb("qp", [P, KC, GROUP], F32)
        k_t = sb("k_t", [P, HID], F32)
        k_e = sb("k_e", [P, HID], F32)
        k_r = sb("k_r", [P, HID], F32)
        kp = sb("kp", [P, 2, HID], F32)
        v_one = sb("v_one", [P, 2, KC, P + 1], F32)
        q_e = sb("q_e", [P, GROUP], F32)
        q_r = sb("q_r", [P, GROUP], F32)
        den, rec, qn_f = k_t, k_e, k_r
        y_t = kp
        kv = sb("kv", [P, BATCHES, KC, P + 1], F32)
        ident = sb("ident", [P, P], F32)
        same_head = sb("same_head", [P, P], F32)
        kb_row = sb("kb_row", [P, HID], F32)
        vb_row = sb("vb_row", [P, HID], F32)
        obga = sb("obga", [P, BATCHES, HID], F32)
        ga_row = sb("ga_row", [P, BATCHES, HID], F32)
        gb_row = sb("gb_row", [P, BATCHES, HID], F32)
        qb_col = sb("qb_col", [P, KC], F32)
        qb_neg = sb("qb_neg", [P, KC], F32)
        ct = sb("ct", [P, KC, BATCHES], F32)
        silu_c = sb("silu_c", [P, KC, BATCHES], F32)
        silu_cr = part(work, 2 * tile_w, F32, KC, BATCHES, P)
        mods = sb("mods", [P, 4, KC, BATCHES], F32)
        modm = sb("modm", [P, 4, KC, BATCHES], F32)
        ksq = sb("ksq", [P, BATCHES, KC], F32)
        krec = sb("krec", [P, KC], F32)
        lut_f = sb("lut_f", [P, TABLE], F32)
        lut_s = sb("lut_s", [P, TABLE], F32)
        tab = sb("tab", [P, TABLE], U32)
        tab_x = sb("tab_x", [P, TABLE // 2], U32)
        tab_h = tab[:, :].bitcast(F16).rearrange("p (k h) -> p k h", h=2)
        sc = sb("sc", [P, 56], F32)
        stats = sb("stats", [P, TILES, 6], F32)
        mv = sb("mv", [P, TILES, 2], F32)
        ve = sb("ve", [P, TILES], F32)
        rstd = sb("rstd", [P, TILES], F32)
        nmr = sb("nmr", [P, TILES], F32)
        half = sb("half", [P, TILES], F32)

        bank = [ctx.enter_context(nc.psum_tensor(f"bank{i}", [P, HID], F32)) for i in range(8)]
        qp_dram = nc.dram_tensor("qp_dram", (GROUPS, P, KC * GROUP), F32, kind="Internal").ap()

        c_in, lut_in, rows_in, idx_in, ow_in = (sem(n) for n in ("c_in", "lut_in", "rows_in", "idx_in", "ow_in"))
        raw_in = [sem(f"raw{n}_in") for n in "kvq"]
        mod_in = [sem(f"mod{s}_in") for s in range(6)]
        consts, silu_done, rep_done, cols_done, rows_done, rows_read = (sem(n) for n in (
            "consts", "silu_done", "rep_done", "cols_done", "rows_done", "rows_read"))
        maxed, reduced, dve_step, pool_step, setup_done = (sem(n) for n in (
            "maxed", "reduced", "dve_step", "pool_step", "setup_done"))
        w_split = sem("w_split")
        att_done, attT_done, attT_read, m_done, m_split = (sem(n) for n in (
            "att_done", "attT_done", "attT_read", "m_done", "m_split"))
        x_in = [sem("x_in0"), sem("x_in1")]
        stats_raw, stats_done, ve_done, rstd_done, nmr_done, xn_done = (sem(n) for n in (
            "stats_raw", "stats_done", "ve_done", "rstd_done", "nmr_done", "xn_done"))
        xT_done, h_f_done, h_done = sem("xT_done"), sem("h_f_done"), sem("h_done")
        proj_done = sem("proj_done")
        k_read, k_act, kp_done, v_read, q_act, qp_done = (sem(n) for n in (
            "k_read", "k_act", "kp_done", "v_read", "q_act", "qp_done"))
        kv_done, kv_read = sem("kv_done"), sem("kv_read")
        qp_out = sem("qp_out")
        look = sem("look")
        k_neg, k_pos, q_neg, q_read = (sem(n) for n in ("k_neg", "k_pos", "q_neg", "q_read"))
        a_done = sem("a_done")
        waited = sem("waited")
        x2_in = [sem("x2_in0"), sem("x2_in1")]
        q_in, qs_done, z_done, z_read, rec_done, qn_f_done, qn_hi_done, qn_done = (sem(n) for n in (
            "q_in", "qs_done", "z_done", "z_read", "rec_done", "qn_f_done", "qn_hi_done", "qn_done"))
        o_done, xob_done, x1_done, stats2_raw, stats2_done = (sem(n) for n in (
            "o_done", "xob_done", "x1_done", "stats2_raw", "stats2_done"))
        ve2_done, rstd2_done, nmr2_done, xn2_done = (sem(n) for n in ("ve2_done", "rstd2_done", "nmr2_done", "xn2_done"))
        x2T_done, h2_f_done, h2_done = sem("x2T_done"), sem("h2_f_done"), sem("h2_done")
        gate_done, up_done, silu_g_done, hid_f_done, hid_hi_done, hid_done, down_done = (sem(n) for n in (
            "gate_done", "up_done", "silu_g_done", "hid_f_done", "hid_hi_done", "hid_done", "down_done"))
        y_read, y_done = sem("y_read"), sem("y_done")
        stored = [sem("stored0"), sem("stored1")]

        block = ctx.enter_context(nc.Block())
        xv = x.rearrange("b (g t p) d -> (b g) p t d", t=TILES, p=P)
        ov = out.rearrange("b (g t p) d -> (b g) p t d", t=TILES, p=P)

        def chunked(w, k=KC):
            return w.rearrange("(k p) n -> p k n", k=k)

        def c1(i):
            return sc[:, bass.ds(i, 1)]

        def rows_of(j):
            return P if j < FC - 1 else TAIL

        def wait_apart(eng, s, n):
            eng.wait_ge(s, n)
            eng.sem_inc(waited, 1)

        def all_groups(eng, body):
            with eng.Fori(0, GROUPS // 2 - 1) as pair:
                for par in range(2):
                    body(2 * pair + par, par, True, True)
            body(GROUPS - 2, 0, True, False)
            body(GROUPS - 1, 1, False, False)

        @block.sync
        def _(sp):
            sp.sem_inc(qp_out, 16)
            sp.dma_start(xg[:, 0], xv[0]).then_inc(x_in[0], 16)
            sp.dma_start(ct[:], chunked(cT)).then_inc(c_in, 16)
            sp.dma_start(raw[0], chunked(kwT)).then_inc(raw_in[0], 16)
            for s in (1, 0):
                sp.dma_start(mod_raw[s], chunked(wmod[:, s * HID:(s + 1) * HID])).then_inc(mod_in[s], 16)
            sp.dma_start(raw[1], chunked(vwT)).then_inc(raw_in[1], 16)
            for row, src in ((kb_row[:], kb), (vb_row[:], vb), (obga[:, 0], ob), (obga[:, 1], ob)):
                sp.dma_start(row, src.partition_broadcast(P)).then_inc(rows_in, 16)
            sp.dma_start(qb_col[:], qb).then_inc(rows_in, 16)
            sp.dma_start(raw[2], chunked(qwT)).then_inc(raw_in[2], 16)
            sp.dma_start(lut_f[:], lut.partition_broadcast(P)).then_inc(lut_in, 16)
            for s in (2, 5, 4, 3):
                sp.dma_start(mod_raw[s], chunked(wmod[:, s * HID:(s + 1) * HID])).then_inc(mod_in[s], 16)
            sp.dma_start(xg[:, 1], xv[1]).then_inc(x_in[1], 16)
            sp.wait_ge(w_split, 3)
            sp.wait_ge(rows_done, 4)
            sp.wait_ge(cols_done, 2)
            gu_idx = w_gu[:, :].bitcast(I32).rearrange("p (k w f) -> p k w f", k=KC, w=2)
            sp.dma_start(gu_idx[:, :, 0], chunked(gateT)).then_inc(idx_in, 16)
            sp.dma_start(gu_idx[:, :, 1], chunked(upT)).then_inc(idx_in, 16)
            dn_idx = w_dn[:, :].bitcast(I32).rearrange("p (j n) -> p j n", j=FC)
            full = (FC - 1) * P
            sp.dma_start(dn_idx[:, 0:FC - 1], chunked(downT[0:full, :], FC - 1)).then_inc(idx_in, 16)
            sp.wait_ge(consts, 2)
            sp.dma_start(dn_idx[0:TAIL, FC - 1], downT[full:INTER, :]).then_inc(idx_in, 16)

            def stage_a(g, par, more, load):
                if load:
                    sp.wait_ge(xT_done, 4 * g + 4)
                    sp.dma_start(xg[:, par], xv[g + 2]).then_inc(x_in[par], 16)
                sp.wait_ge(qp_done, 4 * g + 8)
                sp.dma_start(qp_dram[g], qp[:].rearrange("p k n -> p (k n)")).then_inc(qp_out, 16)

            all_groups(sp, stage_a)

            sp.wait_ge(qp_out, 16 * GROUPS + 16)
            sp.dma_start(qp[:].rearrange("p k n -> p (k n)"), qp_dram[0]).then_inc(q_in, 16)
            for par in range(2):
                sp.wait_ge(xT_done, 4 * GROUPS)
                sp.dma_start(xg[:, par], xv[par]).then_inc(x2_in[par], 16)
            sp.wait_ge(a_done, 1)
            sp.dma_start(owt, chunked(owT)).then_inc(ow_in, 16)
            sp.wait_ge(qn_done, 5)
            sp.dma_start(qp[:].rearrange("p k n -> p (k n)"), qp_dram[1]).then_inc(q_in, 16)

            def stage_b(g, par, more, load):
                if load:
                    sp.wait_ge(qn_done, 4 * g + 9)
                    sp.dma_start(qp[:].rearrange("p k n -> p (k n)"), qp_dram[g + 2]).then_inc(q_in, 16)
                sp.wait_ge(y_done, 4 * g + 8)
                sp.dma_start(ov[g], xg[:, par]).then_inc(stored[par], 16)
                if load:
                    sp.wait_ge(stored[par], 16 * (g // 2 + 1))
                    sp.dma_start(xg[:, par], xv[g + 2]).then_inc(x2_in[par], 16)

            all_groups(sp, stage_b)
            for par in range(2):
                sp.wait_ge(stored[par], 16 * GROUPS // 2)

        @block.gpsimd
        def _(pool):
            for s, n in ((h_done, 4), (kp_done, 4), (qp_done, 4), (nmr_done, 2), (h2_done, 4), (nmr2_done, 2), (y_done, 4)):
                pool.sem_inc(s, n)
            step = [0]

            def link(ins):
                step[0] += 1
                ins.then_inc(pool_step, 1)
                pool.wait_ge(pool_step, step[0])

            link(pool.memset(ident[:], 0.0))
            link(pool.affine_select(out=ident[:], in_=ident[:], compare_op=ALU.not_equal, fill=1.0, base=0,
                                    pattern=[[-1, P]], channel_multiplier=1))
            link(pool.memset(same_head[:], 0.0))
            for h in range(P // HEAD):
                link(pool.memset(same_head[HEAD * h:HEAD * h + HEAD, HEAD * h:HEAD * h + HEAD], 1.0))
            link(pool.memset(half[:], -0.5))
            pool.memset(v_one[:, :, :, P:P + 1], 1.0).then_inc(consts, 1)
            pool.wait_ge(consts, 1)
            for n in (S_K, S_H1, S_H2, S_V, S_Q, S_LUT):
                pool.wait_ge(maxed, 1 + (S_K, S_H1, S_H2, S_V, S_Q, S_LUT).index(n))
                pool.partition_all_reduce(c1(C_AMAX + n), c1(C_MAX + n), P, RMAX).then_inc(reduced, 1)
                if n == S_Q:
                    pool.wait_ge(w_split, 3)
                    pool.memset(w_dn[TAIL // 32 * 32:P, (FC - 1) * HID:FC * HID], 0).then_inc(consts, 1)
                    pool.wait_ge(consts, 2)

            def norm(n, ready, s_ve, s_rstd, s_nmr):
                wait_apart(pool, ready, 4 * n + 4)
                pool.tensor_scalar(ve[:], mv[:, :, 1], 1.0, LN_EPS, ALU.mult, ALU.add).then_inc(s_ve, 1)
                pool.wait_ge(s_ve, n + 1)
                pool.tensor_tensor(rstd[:], ve[:], half[:], ALU.pow).then_inc(s_rstd, 1)
                wait_apart(pool, s_rstd, n + 1)
                pool.tensor_scalar(nmr[:], mv[:, :, 0], -1.0, 0.0, ALU.mult, ALU.add).then_inc(s_nmr, 1)
                pool.wait_ge(s_nmr, 2 * n + 3)
                pool.tensor_tensor(nmr[:], nmr[:], rstd[:], ALU.mult).then_inc(s_nmr, 1)
                wait_apart(pool, s_nmr, 2 * n + 4)

            def xn_a(n, par):
                norm(n, stats_done, ve_done, rstd_done, nmr_done)
                for t in range(TILES):
                    pool.tensor_scalar(xg[:, par, t], xg[:, par, t], rstd[:, t:t + 1], nmr[:, t:t + 1],
                                       ALU.mult, ALU.add).then_inc(xn_done, 1)

            def h_lo_a(n, par, c):
                pool.wait_ge(h_f_done, 4 * n + c + 5)
                pool.tensor_tensor(h_lo[:, par, c], h_f[:, c % 2], h_hi[:, par, c], ALU.subtract).then_inc(h_done, 1)

            def kp_out(g, t):
                pool.wait_ge(k_act, 4 * g + t + 1)
                pool.wait_ge(kv_done, 4 * g + t + 3)
                pool.tensor_tensor(kp[:, t % 2], k_e[:], k_r[:], ALU.add).then_inc(kp_done, 1)

            def qp_store(g, c):
                pool.wait_ge(q_act, 4 * g + c + 1)
                if c == 0:
                    pool.wait_ge(qp_out, 16 * g + 16)
                pool.tensor_tensor(qp[:, c], q_e[:], q_r[:], ALU.add).then_inc(qp_done, 1)

            def stage_a(g, par, more, load):
                for o in range(OUTS):
                    if o < 2 * TILES and o % 2 == 1:
                        kp_out(g, o // 2)
                    if more and o == 4:
                        xn_a(g + 1, 1 - par)
                    if o >= 2 * TILES:
                        qp_store(g, o - 2 * TILES)
                    if more and 7 <= o < 11:
                        h_lo_a(g + 1, 1 - par, o - 7)

            xn_a(0, 0)
            for c in range(KC):
                h_lo_a(0, 0, c)
            all_groups(pool, stage_a)

            for b in range(BATCHES):
                pool.wait_ge(maxed, 7 + b)
                pool.partition_all_reduce(c1(C_AMAX + S_M0 + b), c1(C_MAX + S_M0 + b), P, RMAX).then_inc(reduced, 1)

            def attn(n, par):
                for t in range(TILES):
                    if t == 0:
                        pool.wait_ge(x2_in[par], 16 * (n // 2 + 1))
                    pool.tensor_tensor(xg[:, par, t], xg[:, par, t], obga[:, n // PER_BATCH], ALU.add).then_inc(xob_done, 1)
                norm(n, stats2_done, ve2_done, rstd2_done, nmr2_done)
                wait_apart(pool, x2T_done, 4 * n + 4)
                for t in range(TILES):
                    pool.tensor_scalar(xn2[:, t], xg[:, par, t], rstd[:, t:t + 1], nmr[:, t:t + 1],
                                       ALU.mult, ALU.add).then_inc(xn2_done, 1)
                for c in range(KC):
                    pool.wait_ge(h2_f_done, 4 * n + c + 5)
                    pool.tensor_tensor(h_lo[:, par, c], h_f[:, c % 2], h_hi[:, par, c], ALU.subtract).then_inc(h2_done, 1)

            def stage_b(g, par, more, load):
                if more:
                    attn(g + 1, 1 - par)
                for t in range(TILES):
                    pool.wait_ge(y_read, 4 * g + t + 5)
                    pool.tensor_tensor(xg[:, par, t], xg[:, par, t], y_t[:, t % 2], ALU.add).then_inc(y_done, 1)

            pool.wait_ge(m_split, 2)
            attn(0, 0)
            all_groups(pool, stage_b)

        @block.scalar
        def _(act):
            for s, n in ((h_f_done, 4), (k_pos, 4), (q_read, 4), (h2_f_done, 4), (silu_g_done, 1)):
                act.sem_inc(s, n)
            act.wait_ge(c_in, 16)
            act.activation(silu_c[:], ct[:], ACT.Silu).then_inc(silu_done, 1)

            def h_chunk(n, par, c, xT, h_f_sem, scale, bias):
                act.activation(h_hi[:, par, c], bank[c % 2][:], ACT.Identity, bias=bias, scale=scale)
                act.activation(h_f[:, c % 2], bank[c % 2][:], ACT.Identity, bias=bias, scale=scale).then_inc(h_f_sem, 1)

            def h_a(n, par, c):
                b = n // PER_BATCH
                act.wait_ge(xT_done, 4 * n + c + 1)
                act.wait_ge(h_done, 4 * n + c + 3)
                if c == 0:
                    act.wait_ge(proj_done, OUTS * n + OUTS)
                h_chunk(n, par, c, xT_done, h_f_done, modm[:, 0, c, bass.ds(b, 1)], modm[:, 1, c, bass.ds(b, 1)])

            def v_out(g, t):
                act.wait_ge(proj_done, OUTS * g + 2 * t + 2 + 2 * OUTS)
                act.wait_ge(kv_done, 4 * g + t + 3)
                act.activation(v_one[:, t % 2, :, 0:P],
                               bank[2 + (2 * t + 1) % 4][:].rearrange("p (k n) -> p k n", k=KC),
                               ACT.Copy, scale=c1(C_INV_V)).then_inc(v_read, 1)

            def k_acts(g, t):
                act.wait_ge(k_read, 4 * g + t + 1)
                act.wait_ge(kp_done, 4 * g + t + 4)
                act.activation(k_e[:], k_t[:], ACT.Relu, scale=-1.0).then_inc(k_neg, 1)
                act.activation(k_r[:], k_t[:], ACT.Relu).then_inc(k_pos, 1)
                act.wait_ge(k_neg, 4 * g + t + 1)
                act.activation(k_e[:], k_e[:], ACT.Exp, scale=-1.0).then_inc(k_act, 1)

            def q_acts(g, c):
                act.wait_ge(proj_done, OUTS * g + 2 * TILES + c + 1 + 2 * OUTS)
                act.wait_ge(qp_done, 4 * g + c + 4)
                src = bank[2 + c]
                act.activation(q_e[:], src[:], ACT.Relu, bias=qb_neg[:, c:c + 1], scale=c1(C_NEG_Q)).then_inc(q_neg, 1)
                act.activation(q_r[:], src[:], ACT.Relu, bias=qb_col[:, c:c + 1], scale=c1(C_INV_Q)).then_inc(q_read, 1)
                act.wait_ge(q_neg, 4 * g + c + 1)
                act.activation(q_e[:], q_e[:], ACT.Exp, scale=-1.0).then_inc(q_act, 1)

            def stage_a(g, par, more, load):
                for o in range(OUTS):
                    if o < 2 * TILES and o % 2 == 1:
                        k_acts(g, o // 2)
                        v_out(g, o // 2)
                    if o >= 2 * TILES:
                        q_acts(g, o - 2 * TILES)
                    if more and 6 <= o < 10:
                        h_a(g + 1, 1 - par, o - 6)

            act.wait_ge(setup_done, 1)
            for c in range(KC):
                h_a(0, 0, c)
            act.wait_ge(setup_done, 2)
            all_groups(act, stage_a)

            def h_b(n, par, c):
                b = n // PER_BATCH
                act.wait_ge(x2T_done, 4 * n + c + 5)
                act.wait_ge(h2_done, 4 * n + c + 3)
                if c == 0:
                    act.wait_ge(up_done, FC * n + FC)
                h_chunk(n, par, c, x2T_done, h2_f_done, modm[:, 2, c, bass.ds(b, 1)], modm[:, 3, c, bass.ds(b, 1)])

            def silu_gate(g, j):
                m = rows_of(j)
                act.wait_ge(gate_done, FC * g + j + 1)
                act.wait_ge(hid_f_done, FC * g + FC + (j - 1 if j >= 2 else -j))
                act.activation(silu_g[0:m, j % 2], bank[6][0:m], ACT.Silu, scale=c1(C_INV_G)[0:m]).then_inc(silu_g_done, 1)

            def stage_b(g, par, more, load):
                for j in range(FC):
                    silu_gate(g, j)
                    if more and j in (8, 9):
                        h_b(g + 1, 1 - par, 2 * (j - 8))
                        h_b(g + 1, 1 - par, 2 * (j - 8) + 1)

            for c in range(KC):
                h_b(0, 0, c)
            all_groups(act, stage_b)

        @block.vector
        def _(dve):
            step = [0]

            def link(ins):
                step[0] += 1
                ins.then_inc(dve_step, 1)
                dve.wait_ge(dve_step, step[0])

            A_, M0, M1, M2, M3, B_, C_, D_, E_ = range(9)
            OPS = [
                ("bit", M1, 2, None), ("bit", M2, 4, None), ("bit", M3, 8, None), ("ones", M0, None, None),
                ("leaf", B_, 1, None), ("leaf", A_, 0, None), ("leaf", C_, 2, None), ("leaf", D_, 3, None),
                ("pick", A_, M1, B_), ("pick", C_, M1, D_), ("leaf", B_, 4, None), ("leaf", D_, 5, None),
                ("pick", A_, M2, C_), ("leaf", E_, 7, None), ("pick", B_, M1, D_), ("leaf", C_, 6, None),
                ("pick", C_, M1, E_), ("pick", B_, M2, C_), ("pick", A_, M3, B_), ("store", None, A_, None),
            ]
            needs = [0, 0, 0, 0, 4, 4, 4, 4, 6, 8, 9, 10, 10, 8, 12, 13, 16, 17, 18, 19]
            LOOKS = len(OPS)
            PIECES = 3

            for s, n in ((kv_read, 2), (look, PIECES * LOOKS), (z_read, 4), (rec_done, 1),
                         (qn_f_done, 1), (qn_done, 1), (hid_f_done, FC), (y_read, 4)):
                dve.sem_inc(s, n)

            def pow2(n):
                link(dve.tensor_scalar(c1(C_TMP), c1(C_AMAX + n), 1e-30, None, ALU.max))
                bits = c1(C_TMP).bitcast(U32)
                link(dve.tensor_scalar(c1(C_POW + n).bitcast(U32), bits, EXPONENT, None, ALU.bitwise_and))
                link(dve.tensor_scalar(c1(C_INV + n).bitcast(U32), bits, EXPONENT, EXPONENT,
                                       ALU.bitwise_and, ALU.bitwise_xor))

            def split_weight(i, n):
                link(dve.tensor_scalar(c1(C_SPLIT), c1(C_INV + n), 2.0 ** 13, None, ALU.mult))
                src = raw[i].rearrange("p k n -> p (k n)")
                hi = whi[:, i].rearrange("p k n -> p (k n)")
                link(dve.tensor_scalar(hi, src, c1(C_SPLIT), None, ALU.mult))
                dve.scalar_tensor_tensor(wlo[:, i].rearrange("p k n -> p (k n)"), src, c1(C_SPLIT), hi,
                                         ALU.mult, ALU.subtract).then_inc(w_split, 1)

            def absmax(src, n, s=maxed):
                dve.tensor_reduce(c1(C_MAX + n), src, AX.XYZ if len(src.shape) == 4 else AX.XY if len(src.shape) == 3 else AX.X,
                                  ALU.max, apply_absolute_value=True).then_inc(s, 1)

            def stats_a(n, par):
                dve.wait_ge(x_in[par], 16 * (n // 2 + 1))
                dve.wait_ge(nmr_done, 2 * n + 2)
                for t in range(TILES):
                    dve.bn_stats(stats[:, t], xg[:, par, t]).then_inc(stats_raw, 1)
                for t in range(TILES):
                    wait_apart(dve, stats_raw, 4 * n + t + 1)
                    dve.bn_aggr(mv[:, t], stats[:, t]).then_inc(stats_done, 1)

            stats_a(0, 0)
            dve.wait_ge(silu_done, 1)
            for b in range(BATCHES):
                for k in range(KC):
                    dve.tensor_copy(silu_cr[:, k, b], silu_c[:, k, b:b + 1].to_broadcast([P, P])).then_inc(rep_done, 1)
            dve.wait_ge(raw_in[0], 16)
            absmax(raw[0], S_K)
            dve.wait_ge(cols_done, 1)
            mp = [bank[7 - i][:, 0:2 * KC * BATCHES].rearrange("p (s k b) -> p s k b", s=2, k=KC) for i in range(2)]

            def mod_columns(s, n):
                dve.tensor_scalar(mods[:, s], mp[s // 2][:, 0], 1.0, None, ALU.add)
                link(dve.tensor_scalar(mods[:, s + 1], mp[s // 2][:, 1], 1.0, 0.0, ALU.mult, ALU.add))
                absmax(mods[:, s:s + 2], n)

            def mod_scale(s, n):
                pow2(n)
                link(dve.tensor_scalar(c1(C_SPLIT), c1(C_INV + n), 2.0 ** 8, None, ALU.mult))
                link(dve.tensor_scalar(modm[:, s:s + 2].rearrange("p a b c -> p (a b c)"),
                                       mods[:, s:s + 2].rearrange("p a b c -> p (a b c)"), c1(C_SPLIT), None, ALU.mult))

            def inverse_proj(col, n):
                link(dve.scalar_tensor_tensor(c1(col), c1(C_POW + S_H1), 2.0 ** -23, c1(C_POW + n), ALU.mult, ALU.mult))

            mod_columns(0, S_H1)
            dve.wait_ge(reduced, 1)
            pow2(S_K)
            split_weight(0, S_K)
            dve.wait_ge(reduced, 2)
            mod_scale(0, S_H1)
            inverse_proj(C_INV_K, S_K)
            dve.sem_inc(setup_done, 1)
            dve.wait_ge(cols_done, 2)
            mod_columns(2, S_H2)
            dve.wait_ge(raw_in[1], 16)
            absmax(raw[1], S_V)
            dve.wait_ge(reduced, 4)
            pow2(S_V)
            split_weight(1, S_V)
            inverse_proj(C_INV_V, S_V)
            dve.wait_ge(raw_in[2], 16)
            absmax(raw[2], S_Q)
            dve.wait_ge(reduced, 5)
            pow2(S_Q)
            split_weight(2, S_Q)
            inverse_proj(C_INV_Q, S_Q)
            link(dve.tensor_scalar(c1(C_NEG_Q), c1(C_INV_Q), -1.0, None, ALU.mult))
            dve.wait_ge(rows_in, 5 * 16)
            link(dve.tensor_scalar(qb_neg[:], qb_col[:], -1.0, None, ALU.mult))
            mod_scale(2, S_H2)
            dve.wait_ge(lut_in, 16)
            absmax(lut_f[:], S_LUT)
            dve.wait_ge(reduced, 6)
            pow2(S_LUT)
            link(dve.tensor_scalar(c1(C_SPLIT), c1(C_INV + S_LUT), 2.0 ** 13, None, ALU.mult))
            link(dve.tensor_scalar(lut_s[:], lut_f[:], c1(C_SPLIT), None, ALU.mult))
            link(dve.tensor_copy(tab_h[:, :, 0], lut_s[:]))
            link(dve.tensor_tensor(tab_h[:, :, 1], lut_s[:], tab_h[:, :, 0], ALU.subtract))
            pairs = tab[:, :].rearrange("p (j b) -> p j b", b=2)
            link(dve.tensor_tensor(tab_x[:], pairs[:, :, 0], pairs[:, :, 1], ALU.bitwise_xor))
            e_l, e_h, r_l, r_h = c1(C_POW + S_LUT), c1(C_POW + S_H2), c1(C_INV + S_LUT), c1(C_INV + S_H2)
            link(dve.scalar_tensor_tensor(c1(C_INV_G), e_l, 2.0 ** -23, e_h, ALU.mult, ALU.mult))
            link(dve.scalar_tensor_tensor(c1(C_HID), r_l, 2.0 ** -34, r_h, ALU.mult, ALU.mult))
            link(dve.tensor_tensor(c1(C_TMP), e_l, e_h, ALU.mult))
            link(dve.tensor_tensor(c1(C_TMP + 1), c1(C_TMP), c1(C_TMP), ALU.mult))
            link(dve.scalar_tensor_tensor(c1(C_INV_D), c1(C_TMP + 1), 2.0 ** -5, e_l, ALU.mult, ALU.mult))
            dve.wait_ge(rows_in, 5 * 16)
            for i, row in enumerate((ga_row, gb_row)):
                for b in range(BATCHES):
                    src = bank[2 + 2 * i + b]
                    dve.wait_ge(rows_done, 2 * i + b + 1)
                    t1, t2 = kp[:, 0], kp[:, 1]
                    dve.tensor_scalar(t1, src[:], 0.0, None, ALU.is_ge)
                    link(dve.tensor_scalar(t2.bitcast(U32), src[:].bitcast(U32), MAGNITUDE, None, ALU.bitwise_and))
                    link(dve.tensor_scalar(t1, t1, 2.0, -1.0, ALU.mult, ALU.add))
                    link(dve.scalar_tensor_tensor(row[:, b], t2, 0.25, t1, ALU.max, ALU.mult))
            for b in range(BATCHES):
                link(dve.tensor_tensor(obga[:, b], obga[:, b], ga_row[:, b], ALU.mult))
            for b in range(BATCHES):
                link(dve.memset(kv[:, b].rearrange("p k n -> p (k n)"), 0.0))
            dve.sem_inc(setup_done, 1)

            def lookup_op(g, piece, i):
                kind, dst, a, b = OPS[i]
                if piece < 2:
                    n, word = GU_COLS // 2, w_gu
                    at = g * GU_COLS + piece * n
                else:
                    n, word, at = DN_COLS, w_dn, g * DN_COLS
                dest = word[:, bass.ds(at, n)]

                def buf(k):
                    return lk[k][:, 0:n]

                if piece + needs[i]:
                    dve.wait_ge(look, piece * LOOKS + needs[i])
                if kind == "bit":
                    ins = dve.tensor_scalar(buf(dst), dest, a, None, ALU.bitwise_and)
                elif kind == "ones":
                    ins = dve.tensor_scalar(buf(dst).bitcast(I32), dest.bitcast(I32), 31, 31,
                                            ALU.logical_shift_left, ALU.arith_shift_right)
                elif kind == "leaf":
                    ins = dve.tensor_scalar(buf(dst), buf(M0), tab_x[:, a:a + 1], tab[:, 2 * a:2 * a + 1],
                                            ALU.bitwise_and, ALU.bitwise_xor)
                elif kind == "store":
                    ins = dve.tensor_copy(dest, buf(a))
                else:
                    ins = dve.copy_predicated(buf(dst), buf(a), buf(b))
                ins.then_inc(look, 1)

            def lookup(g, o):
                total = PIECES * LOOKS
                if o == 0:
                    dve.wait_ge(look, total)
                    dve.sem_clear(look)
                for i in range(total * o // OUTS, total * (o + 1) // OUTS):
                    lookup_op(g, i // LOOKS, i % LOOKS)

            def k_out(g, t):
                dve.wait_ge(proj_done, OUTS * g + 2 * t + 1 + 2 * OUTS)
                dve.wait_ge(k_pos, 4 * g + t + 4)
                dve.scalar_tensor_tensor(k_t[:], bank[2 + 2 * t % 4][:], c1(C_INV_K), kb_row[:],
                                         ALU.mult, ALU.add).then_inc(k_read, 1)

            def kv_sum(g):
                dve.wait_ge(kv_done, 4 * g + 8)
                for i in range(2):
                    acc = kv[:, g // PER_BATCH, 2 * i:2 * i + 2]
                    src = kv_bank[i]
                    dve.wait_ge(kv_read, 2 * g + i + 1)
                    dve.tensor_tensor(acc, acc, src, ALU.add).then_inc(kv_read, 1)

            kv_bank = [bank[6 + i][:, 0:2 * (P + 1)].rearrange("p (k n) -> p k n", k=2) for i in range(2)]

            def stage_a(g, par, more, load):
                if more:
                    stats_a(g + 1, 1 - par)
                for o in range(OUTS):
                    if o < 2 * TILES and o % 2 == 0:
                        k_out(g, o // 2)
                    if o == OUTS - 1:
                        kv_sum(g)
                    lookup(g, o)

            dve.wait_ge(idx_in, 4 * 16)
            all_groups(dve, stage_a)
            dve.wait_ge(look, PIECES * LOOKS)
            dve.wait_ge(kv_read, 2 * GROUPS + 2)
            dve.sem_inc(a_done, 1)

            dve.wait_ge(ow_in, 16)
            for b in range(BATCHES):
                link(dve.tensor_scalar(ksq[:, b], kv[:, b, :, P], 1.0 / SEQ, None, ALU.mult))
                link(dve.tensor_scalar(krec[:], kv[:, b, :, P], 1e-30, None, ALU.max))
                link(dve.reciprocal(krec[:], krec[:]))
                if b:
                    dve.wait_ge(attT_done, b)
                for c in range(KC):
                    link(dve.scalar_tensor_tensor(att[:, c], kv[:, b, c, 0:P], krec[:, c:c + 1],
                                                  vb_row[:, c * P:(c + 1) * P], ALU.mult, ALU.add))
                    step[0] += 1
                    dve.tensor_tensor(att[:, c], att[:, c], same_head[:], ALU.mult).then_inc(dve_step, 1)
                dve.wait_ge(dve_step, step[0])
                dve.sem_inc(att_done, 1)
                dve.wait_ge(attT_done, b + 1)
                dve.tensor_copy(att_T, bank[0][:].rearrange("p (k n) -> p k n", k=KC)).then_inc(attT_read, 1)
                for c in range(KC):
                    dve.wait_ge(m_done, b * KC + c + 1)
                    link(dve.tensor_tensor(mfull[:, c], bank[2 + c][:], ga_row[:, b], ALU.mult))
                absmax(mfull, S_M0 + b)
                dve.wait_ge(reduced, 7 + b)
                pow2(S_M0 + b)
                link(dve.tensor_scalar(c1(C_SPLIT), c1(C_INV + S_M0 + b), 2.0 ** 13, None, ALU.mult))
                link(dve.tensor_scalar(c1(C_INV_O + b), c1(C_POW + S_M0 + b), 2.0 ** -29, None, ALU.mult))
                flat = mfull.rearrange("p k n -> p (k n)")
                hi = mhi[:, b].rearrange("p k n -> p (k n)")
                link(dve.tensor_scalar(hi, flat, c1(C_SPLIT), None, ALU.mult))
                dve.scalar_tensor_tensor(mlo[:, b].rearrange("p k n -> p (k n)"), flat, c1(C_SPLIT), hi,
                                         ALU.mult, ALU.subtract).then_inc(m_split, 1)
                dve.wait_ge(m_split, b + 1)

            def qs_all(n):
                dve.wait_ge(q_in, 16 * (n + 1))
                for c in range(KC):
                    dve.tensor_scalar(qp[:, c], qp[:, c], ksq[:, n // PER_BATCH, c:c + 1], None, ALU.mult).then_inc(qs_done, 1)

            def qn_chunk(n, c):
                k = 4 * n + c + 1
                dve.wait_ge(z_done, k)
                dve.wait_ge(rec_done, k)
                dve.tensor_scalar(den[:], bank[c % 2][:], ATTN_EPS / SEQ, None, ALU.add).then_inc(z_read, 1)
                dve.wait_ge(z_read, k + 4)
                dve.wait_ge(qn_f_done, k)
                dve.reciprocal(rec[:], den[:]).then_inc(rec_done, 1)
                dve.wait_ge(rec_done, k + 1)
                dve.wait_ge(qn_done, k)
                dve.scalar_tensor_tensor(qn_f[:], qp[:, c], 2.0 ** 15, rec[:], ALU.mult, ALU.mult).then_inc(qn_f_done, 1)
                dve.wait_ge(qn_f_done, k + 1)
                if c == 0:
                    dve.wait_ge(o_done, 4 * n + 4)
                dve.tensor_copy(qn_hi[:, c], qn_f[:]).then_inc(qn_hi_done, 1)
                dve.wait_ge(qn_hi_done, k)
                dve.tensor_tensor(qn_lo[:, c], qn_f[:], qn_hi[:, c], ALU.subtract).then_inc(qn_done, 1)

            def x1_tile(n, par, t):
                k = 4 * n + t + 1
                dve.wait_ge(o_done, k + 4)
                dve.wait_ge(xob_done, k)
                dve.scalar_tensor_tensor(xg[:, par, t], bank[t % 2][:], c1(C_INV_O + n // PER_BATCH), xg[:, par, t],
                                         ALU.mult, ALU.add).then_inc(x1_done, 1)
                dve.wait_ge(x1_done, k)
                if t == 0:
                    dve.wait_ge(nmr2_done, 2 * n + 2)
                dve.bn_stats(stats[:, t], xg[:, par, t]).then_inc(stats2_raw, 1)
                wait_apart(dve, stats2_raw, k)
                dve.bn_aggr(mv[:, t], stats[:, t]).then_inc(stats2_done, 1)

            def hidden(g, j):
                m, i = rows_of(j), j % 2
                k = FC * g + j + 1
                dve.wait_ge(silu_g_done, k + 1)
                dve.wait_ge(up_done, k + 2 * FC)
                dve.scalar_tensor_tensor(hid_f[0:m, i], bank[7][0:m], c1(C_HID)[0:m], silu_g[0:m, i],
                                         ALU.mult, ALU.mult).then_inc(hid_f_done, 1)
                dve.wait_ge(hid_f_done, k + FC)
                dve.wait_ge(down_done, FC * g + FC + (j - 1 if j >= 2 else -j))
                dve.tensor_copy(hid_hi[0:m, i], hid_f[0:m, i]).then_inc(hid_hi_done, 1)
                dve.wait_ge(hid_hi_done, k)
                dve.tensor_tensor(hid_lo[0:m, i], hid_f[0:m, i], hid_hi[0:m, i], ALU.subtract).then_inc(hid_done, 1)

            def y_tile(g, t):
                k = 4 * g + t + 1
                dve.wait_ge(y_done, k + 2)
                dve.scalar_tensor_tensor(y_t[:, t % 2], bank[2 + t][:], c1(C_INV_D), gb_row[:, g // PER_BATCH],
                                         ALU.mult, ALU.mult).then_inc(y_read, 1)

            def attn_pieces(n, par):
                return {0: [lambda: qn_chunk(n, 0)], 1: [lambda: qn_chunk(n, 1)],
                        2: [lambda: qn_chunk(n, 2)], 3: [lambda: qn_chunk(n, 3)],
                        4: [lambda: x1_tile(n, par, 0)], 5: [lambda: x1_tile(n, par, 1)],
                        6: [lambda: x1_tile(n, par, 2), lambda: x1_tile(n, par, 3)]}

            def stage_b(g, par, more, load):
                if more:
                    qs_all(g + 1)
                for j in range(FC):
                    hidden(g, j)
                    if more:
                        for piece in attn_pieces(g + 1, 1 - par).get(j, ()):
                            piece()
                dve.wait_ge(down_done, FC * g + 2 * FC)
                for t in range(TILES):
                    y_tile(g, t)

            pieces = attn_pieces(0, 0)
            qs_all(0)
            for j in sorted(pieces):
                for piece in pieces[j]:
                    piece()
            all_groups(dve, stage_b)

        @block.tensor
        def _(pe):
            for s, n in ((proj_done, 2 * OUTS), (kv_done, 4), (o_done, 4), (x2T_done, 4),
                         (up_done, 2 * FC), (down_done, FC)):
                pe.sem_inc(s, n)

            def three(dst, pairs, start=True, stop=True):
                last = None
                for i, ((a_hi, a_lo), (b_hi, b_lo)) in enumerate(pairs):
                    first, end = start and i == 0, stop and i == len(pairs) - 1
                    pe.matmul(dst, a_hi, b_hi, start=first, stop=False)
                    pe.matmul(dst, a_hi, b_lo, start=False, stop=False)
                    last = pe.matmul(dst, a_lo, b_hi, start=False, stop=end)
                return last

            def turn(src, n, c, done):
                for t in range(TILES):
                    last = pe.transpose(bank[c % 2][:, t * P:(t + 1) * P], src[:, t, c * P:(c + 1) * P], ident[:])
                last.then_inc(done, 1)

            pe.wait_ge(silu_done, 1)
            for slot, s in ((0, 1), (1, 0), (2, 4), (3, 3)):
                pe.wait_ge(mod_in[s], 16)
                if slot == 2:
                    pe.wait_ge(rep_done, BATCHES * KC)
                    for i, r in enumerate((2, 5)):
                        pe.wait_ge(mod_in[r], 16)
                        for b in range(BATCHES):
                            for k in range(KC):
                                last = pe.matmul(bank[2 + 2 * i + b][:], silu_cr[:, k, b], mod_raw[r][:, k],
                                                 start=(k == 0), stop=(k == KC - 1))
                            last.then_inc(rows_done, 1)
                for c in range(KC):
                    at = (slot % 2 * KC + c) * BATCHES
                    for k in range(KC):
                        last = pe.matmul(bank[7 - slot // 2][:, at:at + BATCHES], mod_raw[s][:, k, c * P:(c + 1) * P], silu_c[:, k],
                                         start=(k == 0), stop=(k == KC - 1), skip_group_check=True)
                if slot % 2:
                    last.then_inc(cols_done, 1)

            def xT_a(n, par, c):
                if c == 0:
                    pe.wait_ge(xn_done, 4 * n + 4)
                pe.wait_ge(h_f_done, 4 * n + c + 3)
                turn(xg[:, par], n, c, xT_done)

            def out_a(g, par, o):
                dst = bank[2 + o % 4]
                h_chunks = [(h_hi[:, par, k], h_lo[:, par, k]) for k in range(KC)]
                if o == 0:
                    pe.wait_ge(h_done, 4 * g + 8)
                if o < 4:
                    pe.wait_ge(q_read, 4 * g + o + 1)
                elif o in (4, 6, 8, 10):
                    pe.wait_ge(k_read, 4 * g + (o - 4) // 2 + 1)
                else:
                    pe.wait_ge(v_read, 4 * g + (o - 5) // 2 + 1)
                if o < 2 * TILES:
                    t, w = o // 2, o % 2
                    pairs = [((hi[:, t * P:(t + 1) * P], lo[:, t * P:(t + 1) * P]), (whi[:, w, k], wlo[:, w, k]))
                             for k, (hi, lo) in enumerate(h_chunks)]
                else:
                    c = o - 2 * TILES
                    pairs = [((whi[:, 2, k, c * P:(c + 1) * P], wlo[:, 2, k, c * P:(c + 1) * P]), (hi, lo))
                             for k, (hi, lo) in enumerate(h_chunks)]
                three(dst[:], pairs).then_inc(proj_done, 1)

            def kv_a(g, t):
                pe.wait_ge(kp_done, 4 * g + t + 5)
                pe.wait_ge(v_read, 4 * g + t + 1)
                if t == 0:
                    pe.wait_ge(kv_read, 2 * g + 2)
                for c in range(KC):
                    n = P + 1
                    at = (c % 2) * n
                    last = pe.matmul(bank[6 + c // 2][:, at:at + n], kp[:, t % 2, c * P:(c + 1) * P], v_one[:, t % 2, c],
                                     start=(t == 0 and c % 2 == 0), stop=(t == TILES - 1), skip_group_check=True)
                last.then_inc(kv_done, 1)

            def stage_a(g, par, more, load):
                for o in range(OUTS):
                    out_a(g, par, o)
                    if o in (3, 5, 7, 9):
                        kv_a(g, (o - 3) // 2)
                    if more and 6 <= o < 10:
                        xT_a(g + 1, 1 - par, o - 6)

            pe.wait_ge(pool_step, 3 + P // HEAD)
            for c in range(KC):
                xT_a(0, 0, c)
            pe.wait_ge(setup_done, 2)
            pe.wait_ge(consts, 1)
            pe.wait_ge(w_split, 3)
            all_groups(pe, stage_a)

            for b in range(BATCHES):
                pe.wait_ge(att_done, b + 1)
                if b:
                    pe.wait_ge(attT_read, b)
                for c in range(KC):
                    last = pe.transpose(bank[0][:, c * P:(c + 1) * P], att[:, c], ident[:])
                last.then_inc(attT_done, 1)
                pe.wait_ge(attT_read, b + 1)
                if b:
                    pe.wait_ge(m_split, b)
                for c in range(KC):
                    pe.matmul(bank[2 + c][:], att_T[:, c], owt[:, c], start=True, stop=True).then_inc(m_done, 1)

            def z_piece(n, c):
                pe.wait_ge(qs_done, 4 * n + c + 1)
                if c < 2:
                    pe.wait_ge(h2_f_done, 4 * n + c + 3)
                else:
                    pe.wait_ge(z_read, 4 * n + c + 3)
                pe.matmul(bank[c % 2][:], same_head[:], qp[:, c], start=True, stop=True).then_inc(z_done, 1)

            def o_piece(n, t):
                if t == 0:
                    pe.wait_ge(qn_done, 4 * n + 5)
                if t < 2:
                    pe.wait_ge(z_read, 4 * n + 3 + t + 4)
                else:
                    pe.wait_ge(x1_done, 4 * n + t - 1)
                b = n // PER_BATCH
                pairs = [((qn_hi[:, c, t * P:(t + 1) * P], qn_lo[:, c, t * P:(t + 1) * P]), (mhi[:, b, c], mlo[:, b, c]))
                         for c in range(KC)]
                three(bank[t % 2][:], pairs).then_inc(o_done, 1)

            def t_piece(n, c):
                if c == 0:
                    pe.wait_ge(xn2_done, 4 * n + 4)
                if c < 2:
                    pe.wait_ge(x1_done, 4 * n + 3 + c)
                else:
                    pe.wait_ge(h2_f_done, 4 * n + c + 3)
                turn(xn2, n, c, x2T_done)

            def gate_up(g, par, j, w, dst):
                m = rows_of(j)
                pairs = [((gu[:, k, w, j * P:j * P + m, 0], gu[:, k, w, j * P:j * P + m, 1]),
                          (h_hi[:, par, k], h_lo[:, par, k])) for k in range(KC)]
                return three(dst[0:m], pairs)

            def down(g, j):
                m, i = rows_of(j), j % 2
                pe.wait_ge(hid_done, FC * g + j + 1)
                if j == 0:
                    pe.wait_ge(y_read, 4 * g + 4)
                for t in range(TILES):
                    pairs = [((hid_hi[0:m, i, t * P:(t + 1) * P], hid_lo[0:m, i, t * P:(t + 1) * P]),
                              (dn[0:m, j, :, 0], dn[0:m, j, :, 1]))]
                    last = three(bank[2 + t][:], pairs, start=(j == 0), stop=(j == FC - 1))
                last.then_inc(down_done, 1)

            BEFORE = {0: ("z", 0), 1: ("z", 2), 8: ("t", 0), 9: ("t", 2)}
            AFTER = {0: ("z", 1), 1: ("z", 3), 4: ("o", 0), 5: ("o", 1), 6: ("o", 2), 7: ("o", 3), 8: ("t", 1), 9: ("t", 3)}

            def piece(which, n, at):
                if at in which:
                    kind, i = which[at]
                    if kind == "z":
                        z_piece(n, i)
                    elif kind == "o":
                        o_piece(n, i)
                    else:
                        t_piece(n, i)

            def stage_b(g, par, more, load):
                for j in range(FC):
                    if j == 0:
                        pe.wait_ge(h2_done, 4 * g + 8)
                    pe.wait_ge(silu_g_done, FC * g + j + 1)
                    gate_up(g, par, j, 0, bank[6]).then_inc(gate_done, 1)
                    if more:
                        piece(BEFORE, g + 1, j)
                    pe.wait_ge(hid_f_done, FC * g + FC + j)
                    gate_up(g, par, j, 1, bank[7]).then_inc(up_done, 1)
                    if j:
                        down(g, j - 1)
                    if more:
                        piece(AFTER, g + 1, j)
                down(g, FC - 1)

            for c in range(KC):
                z_piece(0, c)
            for t in range(TILES):
                o_piece(0, t)
            for c in range(KC):
                t_piece(0, c)
            all_groups(pe, stage_b)


_INS = ["x", "qwT", "qb", "kwT", "kb", "vwT", "vb", "owT", "ob", "lut", "gateT", "upT", "downT", "cT", "wmod"]


def kernel(**inputs):
    import numpy as np
    import concourse.bacc as bacc
    from concourse import mybir as _mybir
    from concourse.bass_utils import run_bass_kernel_spmd

    def t(name):
        return np.ascontiguousarray(np.asarray(inputs[name]).T)

    def a(name):
        return np.ascontiguousarray(np.asarray(inputs[name]))

    laid = dict(
        x=a("L0_attn_hidden_states"),
        qwT=t("L0_attn_q_w"), qb=np.ascontiguousarray(a("L0_attn_q_b").reshape(KC, P).T), kwT=t("L0_attn_k_w"), kb=a("L0_attn_k_b"),
        vwT=t("L0_attn_v_w"), vb=a("L0_attn_v_b"), owT=t("L0_attn_o_w"), ob=a("L0_attn_o_b"),
        lut=a("L0_ffn_lut"), gateT=t("L0_ffn_gate_idx"), upT=t("L0_ffn_up_idx"), downT=t("L0_ffn_down_idx"),
        cT=t("L0_c"), wmod=a("L0_wmod"),
    )
    nc = bacc.Bacc("TRN2", target_bir_lowering=False, num_devices=1)
    arrays, args = {}, []
    for name in _INS:
        arrays[f"in_{name}"] = laid[name]
        args.append(nc.dram_tensor(f"in_{name}", laid[name].shape, _mybir.dt.from_np(laid[name].dtype),
                                   kind="ExternalInput").ap())
    args.append(nc.dram_tensor("out_0", laid["x"].shape, _mybir.dt.float32, kind="ExternalOutput").ap())
    adaln_kernel(nc, *args)
    r = run_bass_kernel_spmd(nc, [arrays], core_ids=[0])
    return r.results[0]["out_0"]
```

```python
from contextlib import ExitStack

import concourse.bass as bass
from concourse import mybir

ALU = mybir.AluOpType
ACT = mybir.ActivationFunctionType
AX = mybir.AxisListType
F32 = mybir.dt.float32
F16 = mybir.dt.float16
U32 = mybir.dt.uint32
I32 = mybir.dt.int32
RMAX = bass.bass_isa.ReduceOp.max

P = 128
BATCHES, SEQ, HID = 2, 2048, 512
HEADS = 16
HEAD = HID // HEADS
INTER = 1376
TABLE = 16
KC = HID // P
GROUP = 512
TILES = GROUP // P
GROUPS = BATCHES * SEQ // GROUP
PER_BATCH = SEQ // GROUP
FC = -(-INTER // P)
TAIL = INTER - (FC - 1) * P
OUTS = 2 * TILES + KC
LN_EPS = 1e-5
ATTN_EPS = 1e-6
EXPONENT, MAGNITUDE = 0x7F800000, 0x7FFFFFFF

PARTS = 3
PIECES = FC * PARTS
LOOK_A, LOOK_A6 = 4, 3
LOOK_B0 = PIECES - 6 * LOOK_A - LOOK_A6
LOOK_STEPS = [
    ("bit", "m1", 2, None, 0), ("bit", "m2", 4, None, 0), ("ones", "m0", None, None, 0),
    ("leaf", "b", 1, None, 3), ("leaf", "r", 0, None, 3), ("leaf", "c", 2, None, 3), ("leaf", "d", 3, None, 3),
    ("pick", "r", "m1", "b", 5), ("pick", "c", "m1", "d", 7), ("leaf", "b", 4, None, 8), ("leaf", "d", 5, None, 9),
    ("pick", "r", "m2", "c", 9), ("pick", "b", "m1", "d", 11), ("leaf", "c", 6, None, 12), ("leaf", "d", 7, None, 13),
    ("bit", "m0", 8, None, 15), ("pick", "c", "m1", "d", 15), ("pick", "b", "m2", "c", 17),
    ("pick", "r", "m0", "b", 18), ("store", None, "r", None, 19),
]
LOOK_BUFS = ("r", "b", "c", "d", "m0", "m1", "m2")
STEPS = len(LOOK_STEPS)

C_MAX, C_AMAX, C_POW, C_INV = 0, 8, 16, 24
S_K, S_V, S_Q, S_H1, S_H2, S_LUT, S_M0, S_M1 = range(8)
C_SPLIT, C_INV_K, C_INV_V, C_INV_Q, C_NEG_Q, C_INV_G, C_HID, C_INV_D, C_INV_O, C_TMP = 32, 33, 34, 35, 36, 37, 38, 39, 40, 42


def adaln_kernel(nc, x, qwT, qb, kwT, kb, vwT, vb, owT, ob, lut, gateT, upT, downT, cT, wmod, out):
    with ExitStack() as ctx:
        def sb(name, shape, dt):
            return ctx.enter_context(nc.sbuf_tensor(name, shape, dt))

        def sem(name):
            return ctx.enter_context(nc.semaphore(name))

        def part(arena, start, dt, *dims):
            n = 1
            for d in dims:
                n *= d
            words = n * (2 if dt == F16 else 4) // 4
            v = arena[:, start:start + words]
            if dt != U32:
                v = v.bitcast(dt)
            if len(dims) == 2:
                v = v.rearrange("p (a b) -> p a b", a=dims[0])
            elif len(dims) == 3:
                v = v.rearrange("p (a b c) -> p a b c", a=dims[0], b=dims[1])
            elif len(dims) == 4:
                v = v.rearrange("p (a b c d) -> p a b c d", a=dims[0], b=dims[1], c=dims[2])
            return v

        tile_w = KC * GROUP
        arena = sb("arena", [P, 4 * tile_w], U32)
        w_ffn = sb("w_ffn", [P, PIECES * GROUP], U32)
        whi = part(arena, tile_w, F16, 3, KC, HID)
        wlo = part(arena, tile_w + 3 * tile_w // 2, F16, 3, KC, HID)
        m_split = part(arena, 0, F16, BATCHES * KC, 2, HID)
        m_full = part(arena, 0, F32, BATCHES * KC, HID)
        xn2 = part(arena, 2 * tile_w, F32, TILES, HID)
        ffn = w_ffn[:, :].bitcast(F16).rearrange("p (j w k n h) -> p j w k n h", j=FC, w=PARTS, k=KC, h=2)
        ffn_idx = w_ffn[:, :].bitcast(I32).rearrange("p (j w k n) -> p j w k n", j=FC, w=PARTS, k=KC)
        look_buf = sb("look_buf", [P, len(LOOK_BUFS), GROUP], U32)
        look_flat = look_buf[:, :, :].rearrange("p a b -> p (a b)")
        raw = [part(w_ffn, i * tile_w, F32, KC, HID) for i in range(3)]
        mod_raw = {m: part(w_ffn, (3 + i) * tile_w, F32, KC, HID) for i, m in enumerate((1, 0, 2, 5, 4))}
        mod_raw[3] = part(look_flat, 0, F32, KC, HID)
        silu_cr = part(arena, 0, F32, KC, BATCHES, P)

        qn = sb("qn", [P, 2, KC, GROUP], F16)
        qn_words = qn[:, :, :, :].rearrange("p a b c -> p (a b c)").bitcast(U32)
        look_wide = ([look_flat[:, i * 2 * GROUP:(i + 1) * 2 * GROUP] for i in range(3)]
                     + [v[:, i * 2 * GROUP:(i + 1) * 2 * GROUP] for v in (arena, qn_words) for i in range(2)])
        owt = [qn_words.bitcast(F32).rearrange("p (k n) -> p k n", k=KC), part(look_flat, 0, F32, KC, HID)]
        hid_f = sb("hid_f", [P, 2, GROUP], F32)
        att_T = [hid_f[:, 0].rearrange("p (k n) -> p k n", k=KC), part(look_flat, tile_w, F32, KC, P)]
        m_tmp = [hid_f[:, 1], part(look_flat, tile_w + HID, F32, 1, HID)[:, 0]]
        xg = sb("xg", [P, 2, TILES, HID], F32)
        h = sb("h", [P, 2, 2, KC, GROUP], F16)
        q0 = h[:, 0].rearrange("p a b c -> p (a b c)").bitcast(F32).rearrange("p (k n) -> p k n", k=KC)
        h_f = sb("h_f", [P, 2, GROUP], F32)
        qp = sb("qp", [P, KC, GROUP], F32)
        shared = sb("shared", [P, 2 * KC * (P + 1) + 5 * GROUP], U32)
        v_w = KC * (P + 1)
        v_one = part(shared, 0, F32, 2, KC, P + 1)
        kp = part(shared, 2 * v_w, F32, 2, HID)
        k_t = part(shared, 2 * v_w + 2 * HID, F32, 1, HID)[:, 0]
        k_e = part(shared, 2 * v_w + 3 * HID, F32, 1, HID)[:, 0]
        q_e = part(shared, 2 * v_w + 4 * HID, F32, 1, HID)[:, 0]
        y_t = part(shared, 0, F32, 2, HID)
        silu_g = part(shared, 2 * HID, F32, 2, GROUP)
        hid = part(shared, 4 * HID, F16, 2, 2, GROUP)
        qn_f = sb("qn_f", [P, 2, GROUP], F32)
        kv = sb("kv", [P, BATCHES, KC, P + 1], F32)
        ident = sb("ident", [P, P], F32)
        same_head = sb("same_head", [P, P], F32)
        kb_row = sb("kb_row", [P, HID], F32)
        vb_row = sb("vb_row", [P, HID], F32)
        obga = sb("obga", [P, BATCHES, HID], F32)
        ga_row = sb("ga_row", [P, BATCHES, HID], F32)
        gb_row = sb("gb_row", [P, BATCHES, HID], F32)
        qb_col = sb("qb_col", [P, KC], F32)
        qb_neg = sb("qb_neg", [P, KC], F32)
        at = tile_w
        ct = part(look_flat, at, F32, KC, BATCHES)
        silu_c = part(look_flat, at + 8, F32, KC, BATCHES)
        mods = part(look_flat, at + 16, F32, 4, KC, BATCHES)
        lut_f = part(look_flat, at + 48, F32, 1, TABLE)[:, 0]
        lut_s = part(look_flat, at + 64, F32, 1, TABLE)[:, 0]
        modm = sb("modm", [P, 4, KC, BATCHES], F32)
        ksq = sb("ksq", [P, BATCHES, KC], F32)
        krec = sb("krec", [P, KC], F32)
        tab = sb("tab", [P, TABLE], U32)
        tab_x = sb("tab_x", [P, TABLE // 2], U32)
        tab_h = tab[:, :].bitcast(F16).rearrange("p (k h) -> p k h", h=2)
        sc = sb("sc", [P, 44], F32)
        stats = sb("stats", [P, TILES, 6], F32)
        mv = sb("mv", [P, TILES, 2], F32)
        ve = sb("ve", [P, TILES], F32)
        rstd = sb("rstd", [P, TILES], F32)
        nmr = sb("nmr", [P, TILES], F32)
        half = sb("half", [P, TILES], F32)

        bank = [ctx.enter_context(nc.psum_tensor(f"bank{i}", [P, HID], F32)) for i in range(8)]
        kv_bank = [bank[6 + i][:, 0:2 * (P + 1)].rearrange("p (k n) -> p k n", k=2) for i in range(2)]
        qp_dram = nc.dram_tensor("qp_dram", (GROUPS, P, KC * GROUP), F32, kind="Internal").ap()

        def sems(names):
            return (sem(n) for n in names.split())

        c_in, lut_in, rows_in, idx_first, idx_rest = sems("c_in lut_in rows_in idx_first idx_rest")
        raw_in = [sem(f"raw{n}_in") for n in "kvq"]
        mod_in = [sem(f"mod{m}_in") for m in range(6)]
        ow_in = [sem("ow0_in"), sem("ow1_in")]
        consts, silu_done, rep_done, cols_done, rows_done, rows_read = sems(
            "consts silu_done rep_done cols_done rows_done rows_read")
        maxed, reduced, dve_step, pool_step, h1_ready, v_ready, q_ready, obga_ready, w_split = sems(
            "maxed reduced dve_step pool_step h1_ready v_ready q_ready obga_ready w_split")
        att_done, attT_done, attT_read, m_done, m_read, m_ready = sems(
            "att_done attT_done attT_read m_done m_read m_ready")
        x_in = [sem("x_in0"), sem("x_in1")]
        stats_raw, stats_done, ve_done, rstd_done, nmr_done, xn_done = sems(
            "stats_raw stats_done ve_done rstd_done nmr_done xn_done")
        xT_done, h_f_done, h_done, proj_done = sems("xT_done h_f_done h_done proj_done")
        k_read, k_neg, k_pos, k_act, kp_done, v_read = sems("k_read k_neg k_pos k_act kp_done v_read")
        q_neg, q_read, q_act, qp_done, qp_out = sems("q_neg q_read q_act qp_done qp_out")
        kv_done, kv_read = sems("kv_done kv_read")
        look, looked = sems("look looked")
        waited = sem("waited")
        q0_in, q_in, qs_done, z_done, z_read, rec_done, qn_f_done, qn_hi_done, qn_done = sems(
            "q0_in q_in qs_done z_done z_read rec_done qn_f_done qn_hi_done qn_done")
        o_done, xob_done, x1_done, stats2_raw, stats2_done, ve2_done, rstd2_done, nmr2_done, xn2_done = sems(
            "o_done xob_done x1_done stats2_raw stats2_done ve2_done rstd2_done nmr2_done xn2_done")
        x2T_done, h2_f_done, h2_done = sems("x2T_done h2_f_done h2_done")
        gate_done, up_done, silu_g_done, hid_f_done, hid_hi_done, hid_done, down_done = sems(
            "gate_done up_done silu_g_done hid_f_done hid_hi_done hid_done down_done")
        y_read, y_done = sems("y_read y_done")
        stored = [sem("stored0"), sem("stored1")]

        block = ctx.enter_context(nc.Block())
        xv = x.rearrange("b (g t p) d -> (b g) p t d", t=TILES, p=P)
        ov = out.rearrange("b (g t p) d -> (b g) p t d", t=TILES, p=P)

        def chunked(w, k=KC):
            return w.rearrange("(k p) n -> p k n", k=k)

        def flat(v):
            return v.rearrange("p k n -> p (k n)")

        def c1(i):
            return sc[:, bass.ds(i, 1)]

        def rows_of(j):
            return P if j < FC - 1 else TAIL

        def last_use(j):
            return j - 1 if j >= 2 else -j

        def wait_apart(eng, s, n):
            eng.wait_ge(s, n)
            eng.sem_inc(waited, 1)

        def run(extra, at):
            for piece in extra.get(at, ()):
                piece()

        def primed(eng, pairs):
            for s, n in pairs:
                eng.sem_inc(s, n)

        @block.sync
        def _(sp):
            primed(sp, ((qp_out, 16),))
            sp.dma_start(ct, chunked(cT)).then_inc(c_in, 16)
            sp.dma_start(lut_f, lut.partition_broadcast(P)).then_inc(lut_in, 16)

            def load_mod(m):
                sp.dma_start(mod_raw[m], chunked(wmod[:, m * HID:(m + 1) * HID])).then_inc(mod_in[m], 16)

            load_mod(1)
            load_mod(0)
            sp.dma_start(xg[:, 0], xv[0]).then_inc(x_in[0], 16)
            sp.dma_start(raw[0], chunked(kwT)).then_inc(raw_in[0], 16)
            load_mod(2)
            load_mod(5)
            sp.dma_start(raw[1], chunked(vwT)).then_inc(raw_in[1], 16)
            for row, src in ((kb_row[:], kb), (vb_row[:], vb), (obga[:, 0], ob), (obga[:, 1], ob)):
                sp.dma_start(row, src.partition_broadcast(P)).then_inc(rows_in, 16)
            sp.dma_start(qb_col[:], qb).then_inc(rows_in, 16)
            load_mod(4)
            load_mod(3)
            sp.dma_start(raw[2], chunked(qwT)).then_inc(raw_in[2], 16)
            sp.dma_start(xg[:, 1], xv[1]).then_inc(x_in[1], 16)

            def load_indices(j, s):
                m = rows_of(j)
                for w, src in ((0, gateT), (1, upT)):
                    sp.dma_start(ffn_idx[:, j, w, :, 0:m], chunked(src[:, j * P:j * P + m])).then_inc(s, 16)
                sp.dma_start(ffn_idx[0:m, j, 2].rearrange("p k n -> p (k n)"), downT[j * P:j * P + m, :]).then_inc(s, 16)

            sp.wait_ge(w_split, 2)
            load_indices(0, idx_first)
            load_indices(1, idx_first)
            sp.wait_ge(w_split, 3)
            sp.wait_ge(rows_done, 4)
            sp.wait_ge(cols_done, 2)
            for j in range(2, FC):
                if j == FC - 1:
                    sp.wait_ge(consts, 2)
                load_indices(j, idx_rest)

            def stage_a(g, par, load):
                if load:
                    sp.wait_ge(xT_done, 4 * g + 4)
                    sp.dma_start(xg[:, par], xv[g + 2]).then_inc(x_in[par], 16)
                sp.wait_ge(qp_done, 4 * g + 8)
                sp.dma_start(qp_dram[g], flat(qp[:])).then_inc(qp_out, 16)

            with sp.Fori(0, 3) as pair:
                for par in range(2):
                    stage_a(2 * pair + par, par, True)
            sp.wait_ge(looked, 1)
            sp.dma_start(owt[0], chunked(owT)).then_inc(ow_in[0], 16)
            sp.wait_ge(xT_done, 4 * 6 + 4)
            sp.dma_start(xg[:, 0], xv[0]).then_inc(x_in[0], 16)
            stage_a(6, 0, False)
            sp.wait_ge(proj_done, OUTS * 7 + 2 * OUTS)
            sp.wait_ge(qp_out, 16 * 7 + 16)
            sp.dma_start(flat(q0), qp_dram[0]).then_inc(q0_in, 16)
            stage_a(7, 1, False)
            sp.wait_ge(qp_out, 16 * 8 + 16)
            sp.dma_start(flat(qp[:]), qp_dram[1]).then_inc(q_in, 16)
            sp.wait_ge(x2T_done, 8)
            sp.dma_start(xg[:, 1], xv[1]).then_inc(x_in[1], 16)

            def stage_b(g, par, load):
                if load:
                    sp.wait_ge(qn_f_done, 4 * g + 8)
                    sp.dma_start(flat(qp[:]), qp_dram[g + 2]).then_inc(q_in, 16)
                sp.wait_ge(y_done, 4 * g + 8)
                sp.dma_start(ov[g], xg[:, par]).then_inc(stored[par], 16)
                if load:
                    sp.wait_ge(stored[par], 16 * (g // 2 + 1))
                    sp.dma_start(xg[:, par], xv[g + 2]).then_inc(x_in[par], 16)

            stage_b(0, 0, True)
            sp.wait_ge(looked, 4)
            sp.dma_start(owt[1], chunked(owT)).then_inc(ow_in[1], 16)
            stage_b(1, 1, True)
            with sp.Fori(0, 2) as pair:
                for par in range(2):
                    stage_b(2 * pair + (2 + par), par, True)
            stage_b(6, 0, False)
            stage_b(7, 1, False)
            for par in range(2):
                sp.wait_ge(stored[par], 16 * GROUPS // 2)

        @block.gpsimd
        def _(pool):
            primed(pool, ((h_done, 4), (kp_done, 4), (qp_done, 4), (nmr_done, 2), (qn_done, 4), (h2_done, 4),
                          (nmr2_done, 2), (hid_done, FC), (y_done, 4)))
            step = [0]

            def link(ins):
                step[0] += 1
                ins.then_inc(pool_step, 1)
                pool.wait_ge(pool_step, step[0])

            link(pool.memset(ident[:], 0.0))
            link(pool.affine_select(out=ident[:], in_=ident[:], compare_op=ALU.not_equal, fill=1.0, base=0,
                                    pattern=[[-1, P]], channel_multiplier=1))
            link(pool.memset(same_head[:], 0.0))
            for i in range(P // HEAD):
                link(pool.memset(same_head[HEAD * i:HEAD * i + HEAD, HEAD * i:HEAD * i + HEAD], 1.0))
            link(pool.memset(half[:], -0.5))
            pool.memset(v_one[:, :, :, P:P + 1], 1.0).then_inc(consts, 1)
            pool.wait_ge(consts, 1)

            def all_max(n, count):
                pool.wait_ge(maxed, count)
                pool.partition_all_reduce(c1(C_AMAX + n), c1(C_MAX + n), P, RMAX).then_inc(reduced, 1)
                pool.wait_ge(reduced, count)

            def norm(n, ready, s_ve, s_rstd, s_nmr):
                wait_apart(pool, ready, 4 * n + 4)
                pool.tensor_scalar(ve[:], mv[:, :, 1], 1.0, LN_EPS, ALU.mult, ALU.add).then_inc(s_ve, 1)
                pool.wait_ge(s_ve, n + 1)
                pool.tensor_tensor(rstd[:], ve[:], half[:], ALU.pow).then_inc(s_rstd, 1)
                wait_apart(pool, s_rstd, n + 1)
                pool.tensor_scalar(nmr[:], mv[:, :, 0], -1.0, 0.0, ALU.mult, ALU.add).then_inc(s_nmr, 1)
                pool.wait_ge(s_nmr, 2 * n + 3)
                pool.tensor_tensor(nmr[:], nmr[:], rstd[:], ALU.mult).then_inc(s_nmr, 1)
                wait_apart(pool, s_nmr, 2 * n + 4)

            def xn_a(n, par):
                norm(n, stats_done, ve_done, rstd_done, nmr_done)
                for t in range(TILES):
                    pool.tensor_scalar(xg[:, par, t], xg[:, par, t], rstd[:, t:t + 1], nmr[:, t:t + 1],
                                       ALU.mult, ALU.add).then_inc(xn_done, 1)

            def h_lo_a(n, par, c):
                pool.wait_ge(h_f_done, 4 * n + c + 5)
                pool.tensor_tensor(h[:, par, 1, c], h_f[:, c % 2], h[:, par, 0, c], ALU.subtract).then_inc(h_done, 1)

            def kp_out(g, t):
                pool.wait_ge(k_act, 4 * g + t + 1)
                pool.tensor_tensor(kp[:, t % 2], k_e, kp[:, t % 2], ALU.add).then_inc(kp_done, 1)

            def qp_sum(g, c):
                pool.wait_ge(q_act, 4 * g + c + 1)
                pool.tensor_tensor(qp[:, c], q_e, qp[:, c], ALU.add).then_inc(qp_done, 1)

            def stage_a(g, par, more, extra={}):
                for o in range(OUTS):
                    if o < 2 * TILES and o % 2 == 1:
                        kp_out(g, o // 2)
                    if more and o == 4:
                        xn_a(g + 1, 1 - par)
                    if o >= 2 * TILES:
                        qp_sum(g, o - 2 * TILES)
                    if more and 7 <= o < 11:
                        h_lo_a(g + 1, 1 - par, o - 7)
                    run(extra, o)

            def qn_lo(n, c):
                k = 4 * n + c + 1
                pool.wait_ge(qn_hi_done, k)
                pool.tensor_tensor(qn[:, 1, c], qn_f[:, c % 2], qn[:, 0, c], ALU.subtract).then_inc(qn_done, 1)

            def xob(n, par):
                wait_apart(pool, x_in[par], 64 + 16 * (n // 2 + 1))
                wait_apart(pool, obga_ready, n // PER_BATCH + 1)
                for t in range(TILES):
                    pool.tensor_tensor(xg[:, par, t], xg[:, par, t], obga[:, n // PER_BATCH], ALU.add).then_inc(xob_done, 1)

            def xn_b(n, par, rows):
                norm(n, stats2_done, ve2_done, rstd2_done, nmr2_done)
                wait_apart(pool, x2T_done, 4 * n + 4)
                for t in range(TILES):
                    pool.tensor_scalar(rows[:, t], xg[:, par, t], rstd[:, t:t + 1], nmr[:, t:t + 1],
                                       ALU.mult, ALU.add).then_inc(xn2_done, 1)

            def h_lo_b(n, par, c):
                pool.wait_ge(h2_f_done, 4 * n + c + 5)
                pool.tensor_tensor(h[:, par, 1, c], h_f[:, c % 2], h[:, par, 0, c], ALU.subtract).then_inc(h2_done, 1)

            all_max(S_LUT, 1)
            xn_a(0, 0)
            pool.wait_ge(xn_done, 4)
            all_max(S_K, 2)
            all_max(S_H1, 3)
            for c in range(KC):
                h_lo_a(0, 0, c)
            pool.wait_ge(h_done, 8)
            all_max(S_V, 4)
            all_max(S_H2, 5)
            all_max(S_Q, 6)
            pool.wait_ge(cols_done, 2)
            pool.memset(w_ffn[:, (FC - 1) * PARTS * GROUP:PIECES * GROUP], 0).then_inc(consts, 1)
            with pool.Fori(0, 3) as pair:
                for par in range(2):
                    stage_a(2 * pair + par, par, True)

            def m0_max():
                pool.wait_ge(kp_done, 4 * 6 + 8)
                all_max(S_M0, 7)

            stage_a(6, 0, True, {7: [m0_max]})
            stage_a(7, 1, False, {2: [lambda: xob(0, 0)], 6: [lambda: qn_lo(0, 0)], 8: [lambda: qn_lo(0, 1)],
                                  10: [lambda: qn_lo(0, 2)]})
            qn_lo(0, 3)
            xn_b(0, 0, xg[:, 1])
            for c in range(KC):
                h_lo_b(0, 0, c)

            def hid_lo(g, j):
                m, i = rows_of(j), j % 2
                pool.wait_ge(hid_hi_done, FC * g + j + 1)
                pool.tensor_tensor(hid[0:m, i, 1], hid_f[0:m, i], hid[0:m, i, 0], ALU.subtract).then_inc(hid_done, 1)

            def stage_b(g, par, more, extra={}):
                n, np = g + 1, 1 - par
                before = {1: [lambda: qn_lo(n, 0)], 2: [lambda: qn_lo(n, 1)], 3: [lambda: qn_lo(n, 2), lambda: xob(n, np)],
                          4: [lambda: qn_lo(n, 3)], 9: [lambda: h_lo_b(n, np, 1)], 10: [lambda: h_lo_b(n, np, 3)]}
                after = {6: [lambda: xn_b(n, np, xn2)], 8: [lambda: h_lo_b(n, np, 0)], 9: [lambda: h_lo_b(n, np, 2)]}
                for j in range(FC):
                    if more:
                        run(before, j)
                    hid_lo(g, j)
                    if more:
                        run(after, j)
                    run(extra, j)
                for t in range(TILES):
                    pool.wait_ge(y_read, 4 * g + t + 5)
                    pool.tensor_tensor(xg[:, par, t], xg[:, par, t], y_t[:, t % 2], ALU.add).then_inc(y_done, 1)

            def m1_max():
                pool.wait_ge(h2_done, 4 * 2 + 4 + 1)
                all_max(S_M1, 8)

            stage_b(0, 0, True)
            stage_b(1, 1, True, {8: [m1_max]})
            with pool.Fori(0, 2) as pair:
                for par in range(2):
                    stage_b(2 * pair + (2 + par), par, True)
            stage_b(6, 0, True)
            stage_b(7, 1, False)

        @block.scalar
        def _(act):
            primed(act, ((h_f_done, 4), (k_pos, 4), (q_read, 4), (z_read, 4), (h2_f_done, 4),
                         (silu_g_done, 1)))
            act.wait_ge(c_in, 16)
            act.activation(silu_c, ct, ACT.Silu).then_inc(silu_done, 1)

            def h_chunk(par, c, h_f_sem, scale, bias):
                act.activation(h[:, par, 0, c], bank[c % 2][:], ACT.Identity, bias=bias, scale=scale)
                act.activation(h_f[:, c % 2], bank[c % 2][:], ACT.Identity, bias=bias, scale=scale).then_inc(h_f_sem, 1)

            def h_a(n, par, c):
                b = n // PER_BATCH
                act.wait_ge(xT_done, 4 * n + c + 1)
                act.wait_ge(h_done, 4 * n + c + 3)
                if c == 0:
                    act.wait_ge(proj_done, OUTS * n + OUTS)
                h_chunk(par, c, h_f_done, modm[:, 0, c, bass.ds(b, 1)], modm[:, 1, c, bass.ds(b, 1)])

            def v_out(g, t):
                act.wait_ge(proj_done, OUTS * g + 2 * t + 2 + 2 * OUTS)
                act.wait_ge(kv_done, 4 * g + t + 3)
                act.activation(v_one[:, t % 2, :, 0:P],
                               bank[2 + (2 * t + 1) % 4][:].rearrange("p (k n) -> p k n", k=KC),
                               ACT.Copy, scale=c1(C_INV_V)).then_inc(v_read, 1)

            def k_acts(g, t):
                act.wait_ge(k_read, 4 * g + t + 1)
                act.wait_ge(kp_done, 4 * g + t + 4)
                act.wait_ge(kv_done, 4 * g + t + 3)
                act.activation(k_e, k_t, ACT.Relu, scale=-1.0).then_inc(k_neg, 1)
                act.activation(kp[:, t % 2], k_t, ACT.Relu).then_inc(k_pos, 1)
                act.wait_ge(k_neg, 4 * g + t + 1)
                act.activation(k_e, k_e, ACT.Exp, scale=-1.0).then_inc(k_act, 1)

            def q_acts(g, c):
                act.wait_ge(proj_done, OUTS * g + 2 * TILES + c + 1 + 2 * OUTS)
                act.wait_ge(qp_done, 4 * g + c + 4)
                if c == 0:
                    act.wait_ge(qp_out, 16 * g + 16)
                src = bank[2 + c]
                act.activation(q_e, src[:], ACT.Relu, bias=qb_neg[:, c:c + 1], scale=c1(C_NEG_Q)).then_inc(q_neg, 1)
                act.activation(qp[:, c], src[:], ACT.Relu, bias=qb_col[:, c:c + 1], scale=c1(C_INV_Q)).then_inc(q_read, 1)
                act.wait_ge(q_neg, 4 * g + c + 1)
                act.activation(q_e, q_e, ACT.Exp, scale=-1.0).then_inc(q_act, 1)

            def stage_a(g, par, more, extra={}):
                for o in range(OUTS):
                    if o < 2 * TILES and o % 2 == 1:
                        k_acts(g, o // 2)
                        v_out(g, o // 2)
                    if o >= 2 * TILES:
                        q_acts(g, o - 2 * TILES)
                    if more and 6 <= o < 10:
                        h_a(g + 1, 1 - par, o - 6)
                    run(extra, o)

            def den(n, c):
                k = 4 * n + c + 1
                act.wait_ge(z_done, k)
                act.wait_ge(qn_done, k + 2)
                act.activation(qn_f[:, c % 2], bank[c % 2][:], ACT.Copy, bias=ATTN_EPS / SEQ).then_inc(z_read, 1)

            def qn_hi(n, c):
                act.wait_ge(qn_f_done, 4 * n + c + 1)
                if c == 0:
                    act.wait_ge(o_done, 4 * n + 4)
                act.activation(qn[:, 0, c], qn_f[:, c % 2], ACT.Copy).then_inc(qn_hi_done, 1)

            def h_b(n, par, c):
                b = n // PER_BATCH
                act.wait_ge(x2T_done, 4 * n + c + 5)
                act.wait_ge(h2_done, 4 * n + c + 3)
                if c == 0:
                    act.wait_ge(up_done, FC * n + FC)
                h_chunk(par, c, h2_f_done, modm[:, 2, c, bass.ds(b, 1)], modm[:, 3, c, bass.ds(b, 1)])

            act.wait_ge(h1_ready, 1)
            for c in range(KC):
                h_a(0, 0, c)
            for i in range(4):
                act.wait_ge(rows_done, i + 1)
                act.activation((ga_row, gb_row)[i // 2][:, i % 2], bank[2 + i][:], ACT.Copy).then_inc(rows_read, 1)
            act.wait_ge(v_ready, 1)
            act.wait_ge(q_ready, 1)
            with act.Fori(0, 3) as pair:
                for par in range(2):
                    stage_a(2 * pair + par, par, True)
            stage_a(6, 0, True)
            stage_a(7, 1, False, {4: [lambda: den(0, 0)], 5: [lambda: den(0, 1)], 6: [lambda: qn_hi(0, 0)],
                                  7: [lambda: den(0, 2)], 8: [lambda: qn_hi(0, 1)], 9: [lambda: den(0, 3)],
                                  10: [lambda: qn_hi(0, 2)]})
            qn_hi(0, 3)
            for c in range(KC):
                h_b(0, 0, c)

            def silu_gate(g, j):
                m = rows_of(j)
                act.wait_ge(gate_done, FC * g + j + 1)
                act.wait_ge(hid_f_done, FC * g + FC + last_use(j))
                act.activation(silu_g[0:m, j % 2], bank[6][0:m], ACT.Silu, scale=c1(C_INV_G)[0:m]).then_inc(silu_g_done, 1)

            def hid_hi(g, j):
                m, i = rows_of(j), j % 2
                act.wait_ge(hid_f_done, FC * g + j + 1 + FC)
                act.wait_ge(down_done, FC * g + FC + last_use(j))
                act.activation(hid[0:m, i, 0], hid_f[0:m, i], ACT.Copy).then_inc(hid_hi_done, 1)

            def stage_b(g, par, more):
                n, np = g + 1, 1 - par
                before = {0: [lambda: den(n, 0)], 1: [lambda: qn_hi(n, 0), lambda: den(n, 1)],
                          2: [lambda: qn_hi(n, 1), lambda: den(n, 2)], 3: [lambda: qn_hi(n, 2), lambda: den(n, 3)],
                          4: [lambda: qn_hi(n, 3)], 8: [lambda: h_b(n, np, 0)], 9: [lambda: h_b(n, np, 2)]}
                after = {8: [lambda: h_b(n, np, 1)], 9: [lambda: h_b(n, np, 3)]}
                for j in range(FC):
                    silu_gate(g, j)
                    if more:
                        run(before, j)
                    hid_hi(g, j)
                    if more:
                        run(after, j)

            stage_b(0, 0, True)
            stage_b(1, 1, True)
            with act.Fori(0, 2) as pair:
                for par in range(2):
                    stage_b(2 * pair + (2 + par), par, True)
            stage_b(6, 0, True)
            stage_b(7, 1, False)

        @block.vector
        def _(dve):
            primed(dve, ((kv_read, 2), (look, LOOK_A // 2 * STEPS), (hid_f_done, FC), (y_read, 4)))
            step = [0]

            def link(ins):
                step[0] += 1
                ins.then_inc(dve_step, 1)
                dve.wait_ge(dve_step, step[0])

            def pow2(n):
                link(dve.tensor_scalar(c1(C_TMP), c1(C_AMAX + n), 1e-30, None, ALU.max))
                bits = c1(C_TMP).bitcast(U32)
                link(dve.tensor_scalar(c1(C_POW + n).bitcast(U32), bits, EXPONENT, None, ALU.bitwise_and))
                link(dve.tensor_scalar(c1(C_INV + n).bitcast(U32), bits, EXPONENT, EXPONENT,
                                       ALU.bitwise_and, ALU.bitwise_xor))

            def absmax(src, n):
                axis = {1: AX.X, 2: AX.XY, 3: AX.XYZ}[len(src.shape) - 1]
                dve.tensor_reduce(c1(C_MAX + n), src, axis, ALU.max, apply_absolute_value=True).then_inc(maxed, 1)

            def weight(i, n, count, col):
                dve.wait_ge(raw_in[i], 16)
                absmax(raw[i], n)
                dve.wait_ge(reduced, count)
                pow2(n)
                link(dve.tensor_scalar(c1(C_SPLIT), c1(C_INV + n), 2.0 ** 13, None, ALU.mult))
                link(dve.tensor_scalar(flat(whi[:, i]), flat(raw[i]), c1(C_SPLIT), None, ALU.mult))
                dve.scalar_tensor_tensor(flat(wlo[:, i]), flat(raw[i]), c1(C_SPLIT), flat(whi[:, i]),
                                         ALU.mult, ALU.subtract).then_inc(w_split, 1)
                if n != S_K:
                    inverse(col, n)

            def inverse(col, n):
                link(dve.scalar_tensor_tensor(c1(col), c1(C_POW + S_H1), 2.0 ** -23, c1(C_POW + n), ALU.mult, ALU.mult))

            def mod_columns(s, n):
                src = bank[7 - s // 2][:, 0:2 * KC * BATCHES].rearrange("p (s k b) -> p s k b", s=2, k=KC)
                dve.tensor_scalar(mods[:, s], src[:, 0], 1.0, None, ALU.add)
                link(dve.tensor_scalar(mods[:, s + 1], src[:, 1], 1.0, 0.0, ALU.mult, ALU.add))
                absmax(mods[:, s:s + 2], n)

            def mod_scale(s, n):
                pow2(n)
                link(dve.tensor_scalar(c1(C_SPLIT), c1(C_INV + n), 2.0 ** 8, None, ALU.mult))
                link(dve.tensor_scalar(modm[:, s:s + 2].rearrange("p a b c -> p (a b c)"),
                                       mods[:, s:s + 2].rearrange("p a b c -> p (a b c)"), c1(C_SPLIT), None, ALU.mult))

            def stats_a(n, par):
                dve.wait_ge(x_in[par], 16 * (n // 2 + 1))
                dve.wait_ge(nmr_done, 2 * n + 2)
                for t in range(TILES):
                    dve.bn_stats(stats[:, t], xg[:, par, t]).then_inc(stats_raw, 1)
                for t in range(TILES):
                    wait_apart(dve, stats_raw, 4 * n + t + 1)
                    dve.bn_aggr(mv[:, t], stats[:, t]).then_inc(stats_done, 1)

            dve.wait_ge(lut_in, 16)
            absmax(lut_f, S_LUT)
            for b in range(BATCHES):
                dve.memset(kv[:, b].rearrange("p k n -> p (k n)"), 0.0).then_inc(dve_step, 1)
                step[0] += 1
            dve.wait_ge(silu_done, 1)
            for b in range(BATCHES):
                for k in range(KC):
                    dve.tensor_copy(silu_cr[:, k, b], silu_c[:, k, b:b + 1].to_broadcast([P, P])).then_inc(rep_done, 1)
            dve.wait_ge(reduced, 1)
            pow2(S_LUT)
            link(dve.tensor_scalar(c1(C_SPLIT), c1(C_INV + S_LUT), 2.0 ** 13, None, ALU.mult))
            link(dve.tensor_scalar(lut_s, lut_f, c1(C_SPLIT), None, ALU.mult))
            link(dve.tensor_copy(tab_h[:, :, 0], lut_s))
            link(dve.tensor_tensor(tab_h[:, :, 1], lut_s, tab_h[:, :, 0], ALU.subtract))
            pairs = tab[:, :].rearrange("p (j b) -> p j b", b=2)
            link(dve.tensor_tensor(tab_x[:], pairs[:, :, 0], pairs[:, :, 1], ALU.bitwise_xor))
            stats_a(0, 0)
            weight(0, S_K, 2, C_INV_K)
            dve.wait_ge(cols_done, 1)
            mod_columns(0, S_H1)
            dve.wait_ge(reduced, 3)
            mod_scale(0, S_H1)
            inverse(C_INV_K, S_K)
            dve.sem_inc(h1_ready, 1)
            weight(1, S_V, 4, C_INV_V)
            dve.sem_inc(v_ready, 1)
            dve.wait_ge(cols_done, 2)
            mod_columns(2, S_H2)
            dve.wait_ge(reduced, 5)
            mod_scale(2, S_H2)
            weight(2, S_Q, 6, C_INV_Q)
            link(dve.tensor_scalar(c1(C_NEG_Q), c1(C_INV_Q), -1.0, None, ALU.mult))
            dve.wait_ge(rows_in, 5 * 16)
            link(dve.tensor_scalar(qb_neg[:], qb_col[:], -1.0, None, ALU.mult))
            e_l, e_h, r_l, r_h = c1(C_POW + S_LUT), c1(C_POW + S_H2), c1(C_INV + S_LUT), c1(C_INV + S_H2)
            link(dve.scalar_tensor_tensor(c1(C_INV_G), e_l, 2.0 ** -23, e_h, ALU.mult, ALU.mult))
            link(dve.scalar_tensor_tensor(c1(C_HID), r_l, 2.0 ** -34, r_h, ALU.mult, ALU.mult))
            link(dve.tensor_tensor(c1(C_TMP), e_l, e_h, ALU.mult))
            link(dve.tensor_tensor(c1(C_TMP + 1), c1(C_TMP), c1(C_TMP), ALU.mult))
            link(dve.scalar_tensor_tensor(c1(C_INV_D), c1(C_TMP + 1), 2.0 ** -5, e_l, ALU.mult, ALU.mult))
            dve.sem_inc(q_ready, 1)

            def clamp(row):
                sign, size = hid_f[:, 0].bitcast(U32), hid_f[:, 1].bitcast(U32)
                link(dve.tensor_scalar(sign.bitcast(F32), row, 0.0, None, ALU.is_ge))
                link(dve.tensor_scalar(size, row.bitcast(U32), MAGNITUDE, None, ALU.bitwise_and))
                link(dve.tensor_scalar(sign.bitcast(F32), sign.bitcast(F32), 2.0, -1.0, ALU.mult, ALU.add))
                link(dve.scalar_tensor_tensor(row, size.bitcast(F32), 0.25, sign.bitcast(F32), ALU.max, ALU.mult))

            def look_step(p, wide, i, done):
                kind, dst, a, b, need = LOOK_STEPS[i]
                words = w_ffn[:, bass.ds(p * GROUP, GROUP * (2 if wide else 1))]

                def buf(k):
                    k = LOOK_BUFS.index(k)
                    return look_wide[k] if wide else look_buf[:, k]

                if done + need:
                    dve.wait_ge(look, done + need)
                if kind == "bit":
                    ins = dve.tensor_scalar(buf(dst), words, a, None, ALU.bitwise_and)
                elif kind == "ones":
                    ins = dve.tensor_scalar(buf(dst).bitcast(I32), words.bitcast(I32), 31, 31,
                                            ALU.logical_shift_left, ALU.arith_shift_right)
                elif kind == "leaf":
                    ins = dve.tensor_scalar(buf(dst), buf("m0"), tab_x[:, a:a + 1], tab[:, 2 * a:2 * a + 1],
                                            ALU.bitwise_and, ALU.bitwise_xor)
                elif kind == "store":
                    ins = dve.tensor_copy(words, buf(a))
                else:
                    ins = dve.copy_predicated(buf(dst), buf(a), buf(b))
                ins.then_inc(look, 1)

            def lookup(first, pieces, wide, before, share, shares):
                step_pieces = 2 if wide else 1
                total = pieces // step_pieces * STEPS
                if share == 0:
                    dve.wait_ge(look, before)
                    dve.sem_clear(look)
                for i in range(total * share // shares, total * (share + 1) // shares):
                    look_step(first + i // STEPS * step_pieces, wide, i % STEPS, i // STEPS * STEPS)

            def k_out(g, t):
                dve.wait_ge(proj_done, OUTS * g + 2 * t + 1 + 2 * OUTS)
                dve.wait_ge(k_pos, 4 * g + t + 4)
                dve.scalar_tensor_tensor(k_t, bank[2 + 2 * t % 4][:], c1(C_INV_K), kb_row[:],
                                         ALU.mult, ALU.add).then_inc(k_read, 1)

            def kv_sum(g):
                dve.wait_ge(kv_done, 4 * g + 8)
                for i in range(2):
                    acc = kv[:, g // PER_BATCH, 2 * i:2 * i + 2]
                    dve.wait_ge(kv_read, 2 * g + i + 1)
                    dve.tensor_tensor(acc, acc, kv_bank[i], ALU.add).then_inc(kv_read, 1)

            def stage_a(g, par, more, pieces=0, wide=False, before=0, first=0, extra={}):
                if more:
                    stats_a(g + 1, 1 - par)
                for o in range(OUTS):
                    run(extra, (o, 0))
                    if o < 2 * TILES and o % 2 == 0:
                        k_out(g, o // 2)
                    run(extra, o)
                    if o == OUTS - 1:
                        kv_sum(g)
                    if pieces:
                        lookup(first, pieces, wide, before, o, OUTS)

            def m_att(b):
                link(dve.tensor_scalar(ksq[:, b], kv[:, b, :, P], 1.0 / SEQ, None, ALU.mult))
                link(dve.tensor_scalar(krec[:], kv[:, b, :, P], 1e-30, None, ALU.max))
                link(dve.reciprocal(krec[:], krec[:]))
                for c in range(KC):
                    a = kv[:, b, c, 0:P]
                    link(dve.scalar_tensor_tensor(a, a, krec[:, c:c + 1], vb_row[:, c * P:(c + 1) * P], ALU.mult, ALU.add))
                    link(dve.tensor_tensor(a, a, same_head[:], ALU.mult))
                dve.sem_inc(att_done, 1)

            def m_attT(b):
                dve.wait_ge(attT_done, b + 1)
                dve.tensor_copy(att_T[b], bank[0][:].rearrange("p (k n) -> p k n", k=KC)).then_inc(attT_read, 1)

            def m_out(b, c):
                dve.wait_ge(m_done, b * KC + c + 1)
                dve.tensor_tensor(m_full[:, b * KC + c], bank[(c + 1) % 2][:], ga_row[:, b], ALU.mult).then_inc(m_read, 1)

            def m_max(b):
                dve.wait_ge(m_read, b * KC + KC)
                absmax(m_full[:, b * KC:b * KC + KC], S_M0 + b)

            def m_scale(b):
                dve.wait_ge(reduced, 7 + b)
                pow2(S_M0 + b)
                link(dve.tensor_scalar(c1(C_SPLIT), c1(C_INV + S_M0 + b), 2.0 ** 13, None, ALU.mult))
                link(dve.tensor_scalar(c1(C_INV_O + b), c1(C_POW + S_M0 + b), 2.0 ** -29, None, ALU.mult))

            def m_cut(b, c):
                c = b * KC + c
                link(dve.tensor_scalar(m_tmp[b], m_full[:, c], c1(C_SPLIT), None, ALU.mult))
                link(dve.tensor_copy(m_split[:, c, 0], m_tmp[b]))
                link(dve.tensor_tensor(m_split[:, c, 1], m_tmp[b], m_split[:, c, 0], ALU.subtract))

            def o_bias(b):
                link(dve.tensor_tensor(obga[:, b], obga[:, b], ga_row[:, b], ALU.mult))
                dve.sem_inc(obga_ready, 1)

            def qs_all(n, q, s, count):
                dve.wait_ge(s, count)
                for c in range(KC):
                    dve.tensor_scalar(q[:, c], q[:, c], ksq[:, n // PER_BATCH, c:c + 1], None, ALU.mult).then_inc(qs_done, 1)

            def qn_full(n, q, c):
                k = 4 * n + c + 1
                dve.wait_ge(z_read, k + 4)
                dve.reciprocal(qn_f[:, c % 2], qn_f[:, c % 2]).then_inc(rec_done, 1)
                dve.wait_ge(rec_done, k)
                dve.scalar_tensor_tensor(qn_f[:, c % 2], q[:, c], 2.0 ** 15, qn_f[:, c % 2],
                                         ALU.mult, ALU.mult).then_inc(qn_f_done, 1)

            def x1_tile(n, par, t):
                k = 4 * n + t + 1
                dve.wait_ge(o_done, k + 4)
                dve.wait_ge(xob_done, k)
                dve.scalar_tensor_tensor(xg[:, par, t], bank[t % 2][:], c1(C_INV_O + n // PER_BATCH), xg[:, par, t],
                                         ALU.mult, ALU.add).then_inc(x1_done, 1)
                dve.wait_ge(x1_done, k)
                if t == 0:
                    dve.wait_ge(nmr2_done, 2 * n + 2)
                dve.bn_stats(stats[:, t], xg[:, par, t]).then_inc(stats2_raw, 1)
                wait_apart(dve, stats2_raw, k)
                dve.bn_aggr(mv[:, t], stats[:, t]).then_inc(stats2_done, 1)

            dve.wait_ge(idx_first, 6 * 16)
            with dve.Fori(0, 3) as pair:
                for par in range(2):
                    g = 2 * pair + par
                    if par:
                        dve.wait_ge(idx_rest, (FC - 2) * 3 * 16)
                    stage_a(g, par, True, LOOK_A, True, LOOK_A // 2 * STEPS, LOOK_A * g)
            dve.wait_ge(look, LOOK_A // 2 * STEPS)
            dve.sem_inc(looked, 1)
            dve.wait_ge(rows_read, 4)
            stage_a(6, 0, True, LOOK_A6, False, LOOK_A // 2 * STEPS, LOOK_A * 6,
                    {(0, 0): [lambda: m_att(0)], 1: [lambda: clamp(ga_row[:, 0])], 2: [lambda: m_attT(0)],
                     4: [lambda: m_out(0, 0)], 5: [lambda: m_out(0, 1)],
                     6: [lambda: m_out(0, 2)], 7: [lambda: m_out(0, 3)], 8: [lambda: m_max(0), lambda: o_bias(0)]})
            dve.wait_ge(look, LOOK_A6 * STEPS)
            dve.sem_inc(looked, 1)
            stage_a(7, 1, False, extra={
                0: [lambda: m_scale(0), lambda: m_cut(0, 0)], 1: [lambda: m_cut(0, 1)], 2: [lambda: qs_all(0, q0, q0_in, 16)],
                3: [lambda: m_cut(0, 2)], 4: [lambda: m_cut(0, 3), lambda: dve.sem_inc(m_ready, 1)],
                5: [lambda: qn_full(0, q0, 0)], 6: [lambda: clamp(ga_row[:, 1])], 7: [lambda: qn_full(0, q0, 1)],
                8: [lambda: o_bias(1), lambda: clamp(gb_row[:, 0])], 10: [lambda: clamp(gb_row[:, 1])], 9: [lambda: qn_full(0, q0, 2)]})
            qn_full(0, q0, 3)
            for t in range(TILES):
                x1_tile(0, 0, t)

            def hid_full(g, j):
                m, i = rows_of(j), j % 2
                k = FC * g + j + 1
                dve.wait_ge(silu_g_done, k + 1)
                dve.wait_ge(up_done, k + 2 * FC)
                dve.wait_ge(hid_done, FC * g + FC + last_use(j))
                dve.scalar_tensor_tensor(hid_f[0:m, i], bank[7][0:m], c1(C_HID)[0:m], silu_g[0:m, i],
                                         ALU.mult, ALU.mult).then_inc(hid_f_done, 1)

            def y_tile(g, t):
                k = 4 * g + t + 1
                dve.wait_ge(y_done, k + 2)
                dve.scalar_tensor_tensor(y_t[:, t % 2], bank[2 + t][:], c1(C_INV_D), gb_row[:, g // PER_BATCH],
                                         ALU.mult, ALU.mult).then_inc(y_read, 1)

            def stage_b(g, par, more, load, looks=False, extra={}, early={}):
                n, np = g + 1, 1 - par
                before = {5: [lambda: x1_tile(n, np, 1)], 6: [lambda: x1_tile(n, np, 3)]}
                after = {0: [lambda: qn_full(n, qp, 0)], 1: [lambda: qn_full(n, qp, 1)], 2: [lambda: qn_full(n, qp, 2)],
                         3: [lambda: qn_full(n, qp, 3)], 4: [lambda: x1_tile(n, np, 0)], 5: [lambda: x1_tile(n, np, 2)]}
                for j in range(FC):
                    if more:
                        run(before, j)
                    run(early, j)
                    hid_full(g, j)
                    if more:
                        run(after, j)
                    run(extra, j)
                    if load and j == FC - 2:
                        qs_all(n + 1, qp, q_in, 16 * (n + 1))
                    if looks and j < FC - 1:
                        lookup(PIECES - LOOK_B0, LOOK_B0, False, LOOK_A6 * STEPS, j, FC - 1)
                        if j == 5:
                            dve.wait_ge(look, LOOK_B0 // 2 * STEPS)
                            dve.sem_inc(looked, 1)
                        if j == FC - 2:
                            dve.wait_ge(look, LOOK_B0 * STEPS)
                            dve.sem_inc(looked, 1)
                dve.wait_ge(down_done, FC * g + 2 * FC)
                for t in range(TILES):
                    y_tile(g, t)

            qs_all(1, qp, q_in, 16)
            stage_b(0, 0, True, True, True)
            stage_b(1, 1, True, True, extra={
                2: [lambda: m_att(1)], 6: [lambda: m_attT(1)], 7: [lambda: m_out(1, 2), lambda: m_out(1, 3), lambda: m_max(1)],
                8: [lambda: m_scale(1)], 9: [lambda: m_cut(1, 0), lambda: m_cut(1, 1)],
                10: [lambda: m_cut(1, 2), lambda: m_cut(1, 3), lambda: dve.sem_inc(m_ready, 1)]},
                early={7: [lambda: m_out(1, 0), lambda: m_out(1, 1)]})
            with dve.Fori(0, 2) as pair:
                for par in range(2):
                    stage_b(2 * pair + (2 + par), par, True, True)
            stage_b(6, 0, True, False)
            stage_b(7, 1, False, False)

        @block.tensor
        def _(pe):
            primed(pe, ((proj_done, 2 * OUTS), (kv_done, 4), (o_done, 4), (x2T_done, 4), (up_done, 2 * FC), (down_done, FC)))

            def three(dst, pairs, start=True, stop=True):
                last = None
                for i, ((a_hi, a_lo), (b_hi, b_lo)) in enumerate(pairs):
                    first, end = start and i == 0, stop and i == len(pairs) - 1
                    pe.matmul(dst, a_hi, b_hi, start=first, stop=False)
                    pe.matmul(dst, a_hi, b_lo, start=False, stop=False)
                    last = pe.matmul(dst, a_lo, b_hi, start=False, stop=end)
                return last

            def turn(src, c, done):
                for t in range(TILES):
                    last = pe.transpose(bank[c % 2][:, t * P:(t + 1) * P], src[:, t, c * P:(c + 1) * P], ident[:])
                last.then_inc(done, 1)

            def xT_a(n, par, c):
                if c == 0:
                    pe.wait_ge(xn_done, 4 * n + 4)
                pe.wait_ge(h_f_done, 4 * n + c + 3)
                turn(xg[:, par], c, xT_done)

            def out_a(g, par, o):
                if o == 0:
                    pe.wait_ge(h_done, 4 * g + 8)
                if o < 4:
                    pe.wait_ge(q_read, 4 * g + o + 1)
                elif o % 2 == 0:
                    pe.wait_ge(k_read, 4 * g + (o - 4) // 2 + 1)
                else:
                    pe.wait_ge(v_read, 4 * g + (o - 5) // 2 + 1)
                h_chunks = [(h[:, par, 0, k], h[:, par, 1, k]) for k in range(KC)]
                if o < 2 * TILES:
                    t, w = o // 2, o % 2
                    pairs = [((hi[:, t * P:(t + 1) * P], lo[:, t * P:(t + 1) * P]), (whi[:, w, k], wlo[:, w, k]))
                             for k, (hi, lo) in enumerate(h_chunks)]
                else:
                    c = o - 2 * TILES
                    pairs = [((whi[:, 2, k, c * P:(c + 1) * P], wlo[:, 2, k, c * P:(c + 1) * P]), (hi, lo))
                             for k, (hi, lo) in enumerate(h_chunks)]
                three(bank[2 + o % 4][:], pairs).then_inc(proj_done, 1)

            def kv_a(g, t):
                pe.wait_ge(kp_done, 4 * g + t + 5)
                pe.wait_ge(v_read, 4 * g + t + 1)
                if t == 0:
                    pe.wait_ge(kv_read, 2 * g + 2)
                for c in range(KC):
                    n = P + 1
                    at = (c % 2) * n
                    last = pe.matmul(bank[6 + c // 2][:, at:at + n], kp[:, t % 2, c * P:(c + 1) * P], v_one[:, t % 2, c],
                                     start=(t == 0 and c % 2 == 0), stop=(t == TILES - 1), skip_group_check=True)
                last.then_inc(kv_done, 1)

            def stage_a(g, par, more, extra={}, late=False):
                for o in range(OUTS):
                    out_a(g, par, o)
                    if o in (3, 5, 7, 9):
                        kv_a(g, (o - 3) // 2)
                    if more and 6 <= o - late < 10:
                        if late and o == 7:
                            pe.wait_ge(m_read, KC)
                        xT_a(g + 1, 1 - par, o - late - 6)
                    run(extra, o)

            def m_turn(b):
                pe.wait_ge(att_done, b + 1)
                if b == 0:
                    pe.wait_ge(h_f_done, 4 * 6 + 3 + 4)
                else:
                    pe.wait_ge(x1_done, 4 * 2 + 3)
                for c in range(KC):
                    last = pe.transpose(bank[0][:, c * P:(c + 1) * P], kv[:, b, c, 0:P], ident[:])
                last.then_inc(attT_done, 1)

            def m_prod(b, c):
                if c == 0:
                    pe.wait_ge(ow_in[b], 16)
                    pe.wait_ge(attT_read, b + 1)
                    if b == 0:
                        pe.wait_ge(h_f_done, 4 * 6 + 4 + 4)
                    else:
                        pe.wait_ge(x1_done, 4 * 2 + 4)
                elif c > 1:
                    pe.wait_ge(m_read, b * KC + c - 1)
                pe.matmul(bank[(c + 1) % 2][:], att_T[b][:, c], owt[b][:, c], start=True, stop=True).then_inc(m_done, 1)

            def z_piece(n, q, c):
                pe.wait_ge(qs_done, 4 * n + c + 1)
                if c < 2:
                    pe.wait_ge(h2_f_done, 4 * n + c + 3)
                else:
                    pe.wait_ge(z_read, 4 * n + c + 3)
                pe.matmul(bank[c % 2][:], same_head[:], q[:, c], start=True, stop=True).then_inc(z_done, 1)

            def o_piece(n, t):
                b = n // PER_BATCH
                if t == 0:
                    pe.wait_ge(m_ready, b + 1)
                    pe.wait_ge(qn_done, 4 * n + 8)
                if t < 2:
                    pe.wait_ge(z_read, 4 * n + 3 + t + 4)
                else:
                    pe.wait_ge(x1_done, 4 * n + t - 1)
                pairs = [((qn[:, 0, c, t * P:(t + 1) * P], qn[:, 1, c, t * P:(t + 1) * P]),
                          (m_split[:, b * KC + c, 0], m_split[:, b * KC + c, 1])) for c in range(KC)]
                three(bank[t % 2][:], pairs).then_inc(o_done, 1)

            def t_piece(n, rows, c):
                if c == 0:
                    pe.wait_ge(xn2_done, 4 * n + 4)
                if c < 2:
                    pe.wait_ge(x1_done, 4 * n + 3 + c)
                else:
                    pe.wait_ge(h2_f_done, 4 * n + c + 3)
                turn(rows, c, x2T_done)

            def columns(slot, s):
                pe.wait_ge(mod_in[s], 16)
                for c in range(KC):
                    at = (slot % 2 * KC + c) * BATCHES
                    for k in range(KC):
                        last = pe.matmul(bank[7 - slot // 2][:, at:at + BATCHES], mod_raw[s][:, k, c * P:(c + 1) * P], silu_c[:, k],
                                         start=(k == 0), stop=(k == KC - 1), skip_group_check=True)
                if slot % 2:
                    last.then_inc(cols_done, 1)

            def rows(i, s):
                pe.wait_ge(mod_in[s], 16)
                for b in range(BATCHES):
                    for k in range(KC):
                        last = pe.matmul(bank[2 + 2 * i + b][:], silu_cr[:, k, b], mod_raw[s][:, k],
                                         start=(k == 0), stop=(k == KC - 1))
                    last.then_inc(rows_done, 1)

            pe.wait_ge(silu_done, 1)
            columns(0, 1)
            columns(1, 0)
            pe.wait_ge(pool_step, 3 + P // HEAD)
            xT_a(0, 0, 0)
            xT_a(0, 0, 1)
            pe.wait_ge(rep_done, BATCHES * KC)
            rows(0, 2)
            xT_a(0, 0, 2)
            xT_a(0, 0, 3)
            rows(1, 5)
            columns(2, 4)
            columns(3, 3)
            pe.wait_ge(rows_read, 4)

            pe.wait_ge(w_split, 3)
            pe.wait_ge(reduced, 5)
            with pe.Fori(0, 3) as pair:
                for par in range(2):
                    stage_a(2 * pair + par, par, True)
            stage_a(6, 0, True, {1: [lambda: m_turn(0)], 3: [lambda: m_prod(0, 0)], 4: [lambda: m_prod(0, 1)],
                                 5: [lambda: m_prod(0, 2)], 6: [lambda: m_prod(0, 3)]}, late=True)
            stage_a(7, 1, False, {2: [lambda: pe.wait_ge(h_f_done, 4 * 8 + 4)],
                                  3: [lambda: z_piece(0, q0, 0)], 4: [lambda: z_piece(0, q0, 1)],
                                  6: [lambda: z_piece(0, q0, 2)], 8: [lambda: z_piece(0, q0, 3)]})
            for t in range(TILES):
                o_piece(0, t)
            for c in range(KC):
                t_piece(0, xg[:, 1], c)

            def gate_up(g, par, j, w, dst):
                m = rows_of(j)
                pairs = [((ffn[:, j, w, k, 0:m, 0], ffn[:, j, w, k, 0:m, 1]), (h[:, par, 0, k], h[:, par, 1, k]))
                         for k in range(KC)]
                return three(dst[0:m], pairs)

            def gate(g, par, j):
                if j == 0:
                    pe.wait_ge(h2_done, 4 * g + 8)
                pe.wait_ge(silu_g_done, FC * g + j + 1)
                gate_up(g, par, j, 0, bank[6]).then_inc(gate_done, 1)

            def up(g, par, j):
                pe.wait_ge(hid_f_done, FC * g + FC + j)
                gate_up(g, par, j, 1, bank[7]).then_inc(up_done, 1)

            def down(g, j):
                m, i = rows_of(j), j % 2
                pe.wait_ge(hid_done, FC * g + j + 1 + FC)
                if j == 0:
                    pe.wait_ge(y_read, 4 * g + 4)
                w_down = ffn[:, j, 2].rearrange("p k n h -> p (k n) h")
                for t in range(TILES):
                    pairs = [((hid[0:m, i, 0, t * P:(t + 1) * P], hid[0:m, i, 1, t * P:(t + 1) * P]),
                              (w_down[0:m, :, 0], w_down[0:m, :, 1]))]
                    last = three(bank[2 + t][:], pairs, start=(j == 0), stop=(j == FC - 1))
                last.then_inc(down_done, 1)

            def stage_b(g, par, more, before={}, after={}, looks=False):
                n, np = g + 1, 1 - par
                b_attn = {0: [lambda: z_piece(n, qp, 0)], 1: [lambda: z_piece(n, qp, 1)], 2: [lambda: z_piece(n, qp, 2)],
                          3: [lambda: z_piece(n, qp, 3)], 5: [lambda: o_piece(n, 1)], 6: [lambda: o_piece(n, 3)],
                          8: [lambda: t_piece(n, xn2, 0)], 9: [lambda: t_piece(n, xn2, 2)]}
                a_attn = {4: [lambda: o_piece(n, 0)], 5: [lambda: o_piece(n, 2)], 8: [lambda: t_piece(n, xn2, 1)],
                          9: [lambda: t_piece(n, xn2, 3)]}
                for j in range(FC):
                    if looks and j >= FC - 2:
                        pe.wait_ge(looked, j - (FC - 2) + 3)
                    if j:
                        gate(g, par, j)
                    run(before, j)
                    if more:
                        run(b_attn, j)
                    up(g, par, j)
                    if j:
                        down(g, j - 1)
                    if more:
                        run(a_attn, j)
                    run(after, j)
                if more:
                    gate(g + 1, np, 0)
                down(g, FC - 1)

            pe.wait_ge(looked, 2)
            pe.wait_ge(kv_read, 2 * GROUPS + 2)
            pe.wait_ge(q_read, 4 * GROUPS + 4)
            gate(0, 0, 0)
            stage_b(0, 0, True, looks=True)
            stage_b(1, 1, True,
                    {7: [lambda: m_prod(1, 0), lambda: m_prod(1, 1)], 8: [lambda: pe.wait_ge(m_read, 2 * KC)]},
                    {6: [lambda: m_turn(1)], 7: [lambda: m_prod(1, 2), lambda: m_prod(1, 3)]})
            with pe.Fori(0, 2) as pair:
                for par in range(2):
                    stage_b(2 * pair + (2 + par), par, True)
            stage_b(6, 0, True)
            stage_b(7, 1, False)


_INS = ["x", "qwT", "qb", "kwT", "kb", "vwT", "vb", "owT", "ob", "lut", "gateT", "upT", "downT", "cT", "wmod"]


def kernel(**inputs):
    import numpy as np
    import concourse.bacc as bacc
    from concourse import mybir as _mybir
    from concourse.bass_utils import run_bass_kernel_spmd

    def t(name):
        return np.ascontiguousarray(np.asarray(inputs[name]).T)

    def a(name):
        return np.ascontiguousarray(np.asarray(inputs[name]))

    laid = dict(
        x=a("L0_attn_hidden_states"),
        qwT=t("L0_attn_q_w"), qb=np.ascontiguousarray(a("L0_attn_q_b").reshape(KC, P).T), kwT=t("L0_attn_k_w"), kb=a("L0_attn_k_b"),
        vwT=t("L0_attn_v_w"), vb=a("L0_attn_v_b"), owT=t("L0_attn_o_w"), ob=a("L0_attn_o_b"),
        lut=a("L0_ffn_lut"), gateT=t("L0_ffn_gate_idx"), upT=t("L0_ffn_up_idx"), downT=t("L0_ffn_down_idx"),
        cT=t("L0_c"), wmod=a("L0_wmod"),
    )
    nc = bacc.Bacc("TRN2", target_bir_lowering=False, num_devices=1)
    arrays, args = {}, []
    for name in _INS:
        arrays[f"in_{name}"] = laid[name]
        args.append(nc.dram_tensor(f"in_{name}", laid[name].shape, _mybir.dt.from_np(laid[name].dtype),
                                   kind="ExternalInput").ap())
    args.append(nc.dram_tensor("out_0", laid["x"].shape, _mybir.dt.float32, kind="ExternalOutput").ap())
    adaln_kernel(nc, *args)
    r = run_bass_kernel_spmd(nc, [arrays], core_ids=[0])
    return r.results[0]["out_0"]
```

```python
from contextlib import ExitStack

import concourse.bass as bass
from concourse import mybir

ALU = mybir.AluOpType
ACT = mybir.ActivationFunctionType
AX = mybir.AxisListType
F32 = mybir.dt.float32
F16 = mybir.dt.float16
U32 = mybir.dt.uint32
I32 = mybir.dt.int32
RMAX = bass.bass_isa.ReduceOp.max

P = 128
BATCHES, SEQ, HID = 2, 2048, 512
HEADS = 16
HEAD = HID // HEADS
INTER = 1376
TABLE = 16
KC = HID // P
GROUP = 512
TILES = GROUP // P
GROUPS = BATCHES * SEQ // GROUP
PER_BATCH = SEQ // GROUP
FC = -(-INTER // P)
TAIL = INTER - (FC - 1) * P
OUTS = 2 * TILES + KC
LN_EPS = 1e-5
ATTN_EPS = 1e-6
EXPONENT, MAGNITUDE = 0x7F800000, 0x7FFFFFFF

PARTS = 3
PIECES = FC * PARTS
LOOK_0, LOOK_PAIR, LOOK_5, LOOK_6, LOOK_7 = 5, 7, 4, 3, 3
LOOK_A = LOOK_0 + 2 * LOOK_PAIR + LOOK_5 + LOOK_6 + LOOK_7
LOOK_B0 = PIECES - LOOK_A
LOOK_STEPS = [
    ("bit", "m1", 2, None, 0), ("bit", "m2", 4, None, 0), ("ones", "m0", None, None, 0),
    ("leaf", "b", 1, None, 3), ("leaf", "r", 0, None, 3), ("leaf", "c", 2, None, 3), ("leaf", "d", 3, None, 3),
    ("pick", "r", "m1", "b", 5), ("pick", "c", "m1", "d", 7), ("leaf", "b", 4, None, 8), ("leaf", "d", 5, None, 9),
    ("pick", "r", "m2", "c", 9), ("pick", "b", "m1", "d", 11), ("leaf", "c", 6, None, 12), ("leaf", "d", 7, None, 13),
    ("bit", "m0", 8, None, 15), ("pick", "c", "m1", "d", 15), ("pick", "b", "m2", "c", 17),
    ("pick", "r", "m0", "b", 18), ("store", None, "r", None, 19),
]
LOOK_BUFS = ("r", "b", "c", "d", "m0", "m1", "m2")
STEPS = len(LOOK_STEPS)

C_MAX, C_AMAX, C_POW, C_INV = 0, 8, 16, 24
S_K, S_V, S_Q, S_H1, S_H2, S_LUT, S_M0, S_M1 = range(8)
C_SPLIT, C_INV_K, C_INV_V, C_INV_Q, C_NEG_Q, C_INV_G, C_HID, C_INV_D, C_INV_O, C_TMP = 32, 33, 34, 35, 36, 37, 38, 39, 40, 42


def adaln_kernel(nc, x, qwT, qb, kwT, kb, vwT, vb, owT, ob, lut, gateT, upT, downT, cT, wmod, out):
    with ExitStack() as ctx:
        def sb(name, shape, dt):
            return ctx.enter_context(nc.sbuf_tensor(name, shape, dt))

        def sem(name):
            return ctx.enter_context(nc.semaphore(name))

        def part(arena, start, dt, *dims):
            n = 1
            for d in dims:
                n *= d
            words = n * (2 if dt == F16 else 4) // 4
            v = arena[:, start:start + words]
            if dt != U32:
                v = v.bitcast(dt)
            if len(dims) == 2:
                v = v.rearrange("p (a b) -> p a b", a=dims[0])
            elif len(dims) == 3:
                v = v.rearrange("p (a b c) -> p a b c", a=dims[0], b=dims[1])
            elif len(dims) == 4:
                v = v.rearrange("p (a b c d) -> p a b c d", a=dims[0], b=dims[1], c=dims[2])
            return v

        tile_w = KC * GROUP
        arena = sb("arena", [P, 4 * tile_w], U32)
        w_ffn = sb("w_ffn", [P, PIECES * GROUP], U32)
        whi = part(arena, tile_w, F16, 3, KC, HID)
        wlo = part(arena, tile_w + 3 * tile_w // 2, F16, 3, KC, HID)
        m_split = part(arena, 0, F16, BATCHES * KC, 2, HID)
        m_full = part(arena, 0, F32, BATCHES * KC, HID)
        xn2 = part(arena, 2 * tile_w, F32, TILES, HID)
        ffn = w_ffn[:, :].bitcast(F16).rearrange("p (j w k n h) -> p j w k n h", j=FC, w=PARTS, k=KC, h=2)
        ffn_idx = w_ffn[:, :].bitcast(I32).rearrange("p (j w k n) -> p j w k n", j=FC, w=PARTS, k=KC)
        look_buf = sb("look_buf", [P, len(LOOK_BUFS), GROUP], U32)
        look_flat = look_buf[:, :, :].rearrange("p a b -> p (a b)")
        raw = [part(w_ffn, i * tile_w, F32, KC, HID) for i in range(3)]
        mod_raw = {m: part(w_ffn, (3 + i) * tile_w, F32, KC, HID) for i, m in enumerate((1, 0, 2, 5, 4))}

        qn = sb("qn", [P, 2, KC, GROUP], F16)
        qn_words = qn[:, :, :, :].rearrange("p a b c -> p (a b c)").bitcast(U32)
        look_wide = ([look_flat[:, i * 2 * GROUP:(i + 1) * 2 * GROUP] for i in range(3)]
                     + [v[:, i * 2 * GROUP:(i + 1) * 2 * GROUP] for v in (arena, qn_words) for i in range(2)])
        owt = [qn_words.bitcast(F32).rearrange("p (k n) -> p k n", k=KC), part(look_flat, 0, F32, KC, HID)]
        hid_f = sb("hid_f", [P, 2, GROUP], F32)
        att_T = [hid_f[:, 0].rearrange("p (k n) -> p k n", k=KC), part(look_flat, tile_w, F32, KC, P)]
        m_tmp = [hid_f[:, 1], part(look_flat, tile_w + HID, F32, 1, HID)[:, 0]]
        xg = sb("xg", [P, 2, TILES, HID], F32)
        h = sb("h", [P, 2, 2, KC, GROUP], F16)
        q0 = h[:, 0].rearrange("p a b c -> p (a b c)").bitcast(F32).rearrange("p (k n) -> p k n", k=KC)
        silu_cr = hid_f[:, :, :].rearrange("p i (k m) -> p (i k) m", k=KC).rearrange("p (k b) m -> p k b m", k=KC)
        h_f = sb("h_f", [P, 2, GROUP], F32)
        qp = sb("qp", [P, KC, GROUP], F32)
        mod_raw[3] = qp[:, :, :]
        shared = sb("shared", [P, 2 * KC * (P + 1) + 5 * GROUP], U32)
        v_w = KC * (P + 1)
        v_one = part(shared, 0, F32, 2, KC, P + 1)
        kp = part(shared, 2 * v_w, F32, 2, HID)
        k_t = part(shared, 2 * v_w + 2 * HID, F32, 1, HID)[:, 0]
        k_e = part(shared, 2 * v_w + 3 * HID, F32, 1, HID)[:, 0]
        q_e = part(shared, 2 * v_w + 4 * HID, F32, 1, HID)[:, 0]
        y_t = part(shared, 0, F32, 2, HID)
        silu_g = part(shared, 2 * HID, F32, 2, GROUP)
        hid = part(shared, 4 * HID, F16, 2, 2, GROUP)
        qn_f = sb("qn_f", [P, 2, GROUP], F32)
        kv = sb("kv", [P, BATCHES, KC, P + 1], F32)
        ident = sb("ident", [P, P], F32)
        same_head = sb("same_head", [P, P], F32)
        kb_row = sb("kb_row", [P, HID], F32)
        vb_row = sb("vb_row", [P, HID], F32)
        obga = sb("obga", [P, BATCHES, HID], F32)
        ga_row = sb("ga_row", [P, BATCHES, HID], F32)
        gb_row = sb("gb_row", [P, BATCHES, HID], F32)
        qb_col = sb("qb_col", [P, KC], F32)
        qb_neg = sb("qb_neg", [P, KC], F32)
        at = 3 * 2 * GROUP
        ct = part(look_flat, at, F32, KC, BATCHES)
        silu_c = part(look_flat, at + 8, F32, KC, BATCHES)
        mods = part(look_flat, at + 16, F32, 4, KC, BATCHES)
        lut_f = part(look_flat, at + 48, F32, 1, TABLE)[:, 0]
        lut_s = part(look_flat, at + 64, F32, 1, TABLE)[:, 0]
        modm = sb("modm", [P, 4, KC, BATCHES], F32)
        ksq = sb("ksq", [P, BATCHES, KC], F32)
        krec = sb("krec", [P, KC], F32)
        tab = sb("tab", [P, TABLE], U32)
        tab_x = sb("tab_x", [P, TABLE // 2], U32)
        tab_h = tab[:, :].bitcast(F16).rearrange("p (k h) -> p k h", h=2)
        sc = sb("sc", [P, 44], F32)
        stats = sb("stats", [P, TILES, 6], F32)
        mv = sb("mv", [P, TILES, 2], F32)
        ve = sb("ve", [P, TILES], F32)
        rstd = sb("rstd", [P, TILES], F32)
        nmr = sb("nmr", [P, TILES], F32)
        half = sb("half", [P, TILES], F32)

        bank = [ctx.enter_context(nc.psum_tensor(f"bank{i}", [P, HID], F32)) for i in range(8)]
        kv_bank = [bank[6 + i][:, 0:2 * (P + 1)].rearrange("p (k n) -> p k n", k=2) for i in range(2)]
        qp_dram = nc.dram_tensor("qp_dram", (GROUPS, P, KC * GROUP), F32, kind="Internal").ap()

        def sems(names):
            return (sem(n) for n in names.split())

        c_in, lut_in, rows_in, idx_first, idx_rest = sems("c_in lut_in rows_in idx_first idx_rest")
        raw_in = [sem(f"raw{n}_in") for n in "kvq"]
        mod_in = [sem(f"mod{m}_in") for m in range(6)]
        ow_in = [sem("ow0_in"), sem("ow1_in")]
        consts, silu_done, rep_done, cols_done, rows_done, rows_read = sems(
            "consts silu_done rep_done cols_done rows_done rows_read")
        maxed, reduced, dve_step, pool_step, h1_ready, v_ready, q_ready, obga_ready, w_split = sems(
            "maxed reduced dve_step pool_step h1_ready v_ready q_ready obga_ready w_split")
        att_done, attT_done, attT_read, m_done, m_read, m_ready = sems(
            "att_done attT_done attT_read m_done m_read m_ready")
        x_in = [sem("x_in0"), sem("x_in1")]
        stats_raw, stats_done, ve_done, rstd_done, nmr_done, xn_done = sems(
            "stats_raw stats_done ve_done rstd_done nmr_done xn_done")
        xT_done, h_f_done, h_done, proj_done = sems("xT_done h_f_done h_done proj_done")
        k_read, k_biased, k_neg, k_pos, k_act, kp_done, v_read = sems(
            "k_read k_biased k_neg k_pos k_act kp_done v_read")
        q_neg, q_read, q_act, qp_done, qp_out = sems("q_neg q_read q_act qp_done qp_out")
        kv_done, kv_read = sems("kv_done kv_read")
        look, looked = sems("look looked")
        waited = sem("waited")
        q0_in, q_in, qs_done, z_done, z_read, rec_done, qn_f_done, qn_hi_done, qn_done = sems(
            "q0_in q_in qs_done z_done z_read rec_done qn_f_done qn_hi_done qn_done")
        o_done, xob_done, x1_done, stats2_raw, stats2_done, ve2_done, rstd2_done, nmr2_done, xn2_done = sems(
            "o_done xob_done x1_done stats2_raw stats2_done ve2_done rstd2_done nmr2_done xn2_done")
        x2T_done, h2_f_done, h2_done = sems("x2T_done h2_f_done h2_done")
        gate_done, up_done, silu_g_done, hid_f_done, hid_hi_done, hid_done, down_done = sems(
            "gate_done up_done silu_g_done hid_f_done hid_hi_done hid_done down_done")
        y_read, y_done = sems("y_read y_done")
        stored = [sem("stored0"), sem("stored1")]
        last_sum, last_stored = sems("last_sum last_stored")

        block = ctx.enter_context(nc.Block())
        xv = x.rearrange("b (g t p) d -> (b g) p t d", t=TILES, p=P)
        ov = out.rearrange("b (g t p) d -> (b g) p t d", t=TILES, p=P)

        def chunked(w, k=KC):
            return w.rearrange("(k p) n -> p k n", k=k)

        def flat(v):
            return v.rearrange("p k n -> p (k n)")

        def c1(i):
            return sc[:, bass.ds(i, 1)]

        def rows_of(j):
            return P if j < FC - 1 else TAIL

        def last_use(j):
            return j - 1 if j >= 2 else -j

        def wait_apart(eng, s, n):
            eng.wait_ge(s, n)
            eng.sem_inc(waited, 1)

        def run(extra, at):
            for piece in extra.get(at, ()):
                piece()

        XN_SLOT, XT_SLOT, M_LATE = 3, 5, 1
        ROW_BANK, COL_BANK = (4, 5, 0, 1), (7, 0)

        def primed(eng, pairs):
            for s, n in pairs:
                eng.sem_inc(s, n)

        @block.sync
        def _(sp):
            primed(sp, ((qp_out, 16),))
            sp.dma_start(ct, chunked(cT)).then_inc(c_in, 16)
            sp.dma_start(lut_f, lut.partition_broadcast(P)).then_inc(lut_in, 16)

            def load_mod(m):
                sp.dma_start(mod_raw[m], chunked(wmod[:, m * HID:(m + 1) * HID])).then_inc(mod_in[m], 16)

            load_mod(1)
            load_mod(0)
            sp.dma_start(xg[:, 0], xv[0]).then_inc(x_in[0], 16)
            sp.dma_start(raw[0], chunked(kwT)).then_inc(raw_in[0], 16)
            load_mod(2)
            sp.dma_start(raw[1], chunked(vwT)).then_inc(raw_in[1], 16)
            for row, src in ((kb_row[:], kb), (vb_row[:], vb), (obga[:, 0], ob), (obga[:, 1], ob)):
                sp.dma_start(row, src.partition_broadcast(P)).then_inc(rows_in, 16)
            sp.dma_start(qb_col[:], qb).then_inc(rows_in, 16)
            sp.dma_start(raw[2], chunked(qwT)).then_inc(raw_in[2], 16)
            load_mod(5)
            sp.dma_start(xg[:, 1], xv[1]).then_inc(x_in[1], 16)
            load_mod(4)
            load_mod(3)

            def load_indices(j, s):
                m = rows_of(j)
                for w, src in ((0, gateT), (1, upT)):
                    sp.dma_start(ffn_idx[:, j, w, :, 0:m], chunked(src[:, j * P:j * P + m])).then_inc(s, 16)
                sp.dma_start(ffn_idx[0:m, j, 2].rearrange("p k n -> p (k n)"), downT[j * P:j * P + m, :]).then_inc(s, 16)

            sp.wait_ge(w_split, 2)
            load_indices(0, idx_first)
            load_indices(1, idx_first)
            sp.wait_ge(w_split, 3)
            for j in (2, 3):
                load_indices(j, idx_rest)
            sp.wait_ge(rows_done, 4)
            sp.wait_ge(cols_done, 2)
            for j in range(4, FC):
                if j == FC - 1:
                    sp.wait_ge(consts, 2)
                load_indices(j, idx_rest)

            def stage_a(g, par, load):
                if load:
                    sp.wait_ge(xT_done, 4 * g + 4)
                    sp.dma_start(xg[:, par], xv[g + 2]).then_inc(x_in[par], 16)
                sp.wait_ge(qp_done, 4 * g + 8)
                sp.dma_start(qp_dram[g], flat(qp[:])).then_inc(qp_out, 16)

            stage_a(0, 0, True)
            with sp.Fori(0, 2) as pair:
                for par in (1, 0):
                    stage_a(2 * pair + (2 - par), par, True)
            stage_a(5, 1, True)
            sp.wait_ge(looked, 1)
            sp.dma_start(owt[0], chunked(owT)).then_inc(ow_in[0], 16)
            sp.wait_ge(xT_done, 4 * 6 + 4)
            sp.dma_start(xg[:, 0], xv[0]).then_inc(x_in[0], 16)
            stage_a(6, 0, False)
            sp.wait_ge(proj_done, OUTS * 7 + 2 * OUTS)
            sp.wait_ge(qp_out, 16 + 16)
            sp.dma_start(flat(q0), qp_dram[0]).then_inc(q0_in, 16)
            stage_a(7, 1, False)
            sp.wait_ge(qp_out, 16 * 8 + 16)
            sp.dma_start(flat(qp[:]), qp_dram[1]).then_inc(q_in, 16)
            sp.wait_ge(x2T_done, 8)
            sp.dma_start(xg[:, 1], xv[1]).then_inc(x_in[1], 16)

            def stage_b(g, par, load, last=False):
                if load:
                    sp.wait_ge(qn_f_done, 4 * g + 8)
                    sp.dma_start(flat(qp[:]), qp_dram[g + 2]).then_inc(q_in, 16)
                if last:
                    for t in range(TILES):
                        sp.wait_ge(y_done, 4 * g + 5 + t)
                        sp.dma_start(ov[g][:, t], xg[:, par, t]).then_inc(last_stored, 16)
                    return
                sp.wait_ge(y_done, 4 * g + 8)
                sp.dma_start(ov[g], xg[:, par]).then_inc(stored[par], 16)
                if load:
                    sp.wait_ge(stored[par], 16 * (g // 2 + 1))
                    sp.dma_start(xg[:, par], xv[g + 2]).then_inc(x_in[par], 16)

            stage_b(0, 0, True)
            sp.wait_ge(looked, 4)
            sp.dma_start(owt[1], chunked(owT)).then_inc(ow_in[1], 16)
            stage_b(1, 1, True)
            with sp.Fori(0, 2) as pair:
                for par in range(2):
                    stage_b(2 * pair + (2 + par), par, True)
            stage_b(6, 0, False)
            stage_b(7, 1, False, last=True)
            for par in range(2):
                sp.wait_ge(stored[par], 16 * (GROUPS // 2 - par))
            sp.wait_ge(last_stored, 16 * TILES)

        @block.gpsimd
        def _(pool):
            primed(pool, ((h_done, 4), (kp_done, 4), (qp_done, 4), (nmr_done, 2), (qn_done, 4), (h2_done, 4),
                          (nmr2_done, 2), (hid_done, FC), (y_done, 4)))
            step = [0]

            def link(ins):
                step[0] += 1
                ins.then_inc(pool_step, 1)
                pool.wait_ge(pool_step, step[0])

            link(pool.memset(ident[:], 0.0))
            link(pool.affine_select(out=ident[:], in_=ident[:], compare_op=ALU.not_equal, fill=1.0, base=0,
                                    pattern=[[-1, P]], channel_multiplier=1))
            link(pool.memset(same_head[:], 0.0))
            for i in range(P // HEAD):
                link(pool.memset(same_head[HEAD * i:HEAD * i + HEAD, HEAD * i:HEAD * i + HEAD], 1.0))
            link(pool.memset(half[:], -0.5))
            pool.memset(v_one[:, :, :, P:P + 1], 1.0).then_inc(consts, 1)
            pool.wait_ge(consts, 1)

            def all_max(n, count):
                pool.wait_ge(maxed, count)
                pool.partition_all_reduce(c1(C_AMAX + n), c1(C_MAX + n), P, RMAX).then_inc(reduced, 1)
                pool.wait_ge(reduced, count)

            def norm(n, ready, s_ve, s_rstd, s_nmr):
                wait_apart(pool, ready, 4 * n + 4)
                pool.tensor_scalar(ve[:], mv[:, :, 1], 1.0, LN_EPS, ALU.mult, ALU.add).then_inc(s_ve, 1)
                pool.wait_ge(s_ve, n + 1)
                pool.tensor_tensor(rstd[:], ve[:], half[:], ALU.pow).then_inc(s_rstd, 1)
                wait_apart(pool, s_rstd, n + 1)
                pool.tensor_scalar(nmr[:], mv[:, :, 0], -1.0, 0.0, ALU.mult, ALU.add).then_inc(s_nmr, 1)
                pool.wait_ge(s_nmr, 2 * n + 3)
                pool.tensor_tensor(nmr[:], nmr[:], rstd[:], ALU.mult).then_inc(s_nmr, 1)
                wait_apart(pool, s_nmr, 2 * n + 4)

            def xn_a(n, par):
                norm(n, stats_done, ve_done, rstd_done, nmr_done)
                for t in range(TILES):
                    pool.tensor_scalar(xg[:, par, t], xg[:, par, t], rstd[:, t:t + 1], nmr[:, t:t + 1],
                                       ALU.mult, ALU.add).then_inc(xn_done, 1)

            def h_lo_a(n, par, c):
                pool.wait_ge(h_f_done, 4 * n + c + 5)
                pool.tensor_tensor(h[:, par, 1, c], h_f[:, c % 2], h[:, par, 0, c], ALU.subtract).then_inc(h_done, 1)

            def k_bias(g, t):
                pool.wait_ge(k_read, 4 * g + t + 1)
                pool.tensor_tensor(k_t, k_t, kb_row[:], ALU.add).then_inc(k_biased, 1)

            def kp_out(g, t):
                pool.wait_ge(k_act, 4 * g + t + 1)
                pool.tensor_tensor(kp[:, t % 2], k_e, kp[:, t % 2], ALU.add).then_inc(kp_done, 1)

            def qp_sum(g, c):
                pool.wait_ge(q_act, 4 * g + c + 1)
                pool.tensor_tensor(qp[:, c], q_e, qp[:, c], ALU.add).then_inc(qp_done, 1)

            def stage_a(g, par, more, extra={}, late=0):
                for o in range(OUTS):
                    if o < 2 * TILES and o % 2 == 0:
                        k_bias(g, o // 2)
                    if o < 2 * TILES and o % 2 == 1:
                        kp_out(g, o // 2)
                    if more and o == XN_SLOT:
                        xn_a(g + 1, 1 - par)
                    if o >= 2 * TILES:
                        qp_sum(g, o - 2 * TILES)
                    if more and 0 <= o - late - XT_SLOT - 1 < KC:
                        h_lo_a(g + 1, 1 - par, o - late - XT_SLOT - 1)
                    run(extra, o)

            def qn_lo(n, c):
                k = 4 * n + c + 1
                pool.wait_ge(qn_hi_done, k)
                pool.tensor_tensor(qn[:, 1, c], qn_f[:, c % 2], qn[:, 0, c], ALU.subtract).then_inc(qn_done, 1)

            def xob(n, par):
                wait_apart(pool, x_in[par], 64 + 16 * (n // 2 + 1))
                wait_apart(pool, obga_ready, n // PER_BATCH + 1)
                for t in range(TILES):
                    pool.tensor_tensor(xg[:, par, t], xg[:, par, t], obga[:, n // PER_BATCH], ALU.add).then_inc(xob_done, 1)

            def xn_b(n, par, rows):
                norm(n, stats2_done, ve2_done, rstd2_done, nmr2_done)
                wait_apart(pool, x2T_done, 4 * n + 4)
                for t in range(TILES):
                    pool.tensor_scalar(rows[:, t], xg[:, par, t], rstd[:, t:t + 1], nmr[:, t:t + 1],
                                       ALU.mult, ALU.add).then_inc(xn2_done, 1)

            def h_lo_b(n, par, c):
                pool.wait_ge(h2_f_done, 4 * n + c + 5)
                pool.tensor_tensor(h[:, par, 1, c], h_f[:, c % 2], h[:, par, 0, c], ALU.subtract).then_inc(h2_done, 1)

            all_max(S_LUT, 1)
            norm(0, stats_done, ve_done, rstd_done, nmr_done)
            all_max(S_K, 2)
            all_max(S_H1, 3)
            all_max(S_V, 4)
            for c in range(KC):
                h_lo_a(0, 0, c)
            pool.wait_ge(h_done, 8)
            all_max(S_Q, 5)

            def h2_max():
                pool.wait_ge(xn_done, 4 * 1 + 4)
                all_max(S_H2, 6)

            def clear_tail():
                pool.wait_ge(cols_done, 2)
                pool.memset(w_ffn[:, (FC - 1) * PARTS * GROUP:PIECES * GROUP], 0).then_inc(consts, 1)

            pool.wait_ge(rows_in, 5 * 16)
            stage_a(0, 0, True, {4: [h2_max, clear_tail]})
            with pool.Fori(0, 2) as pair:
                for par in (1, 0):
                    stage_a(2 * pair + (2 - par), par, True)
            stage_a(5, 1, True)

            def m0_max():
                pool.wait_ge(xn_done, 4 * 7 + 4)
                pool.wait_ge(kp_done, 4 * 6 + 3 + 4)
                pool.wait_ge(k_biased, 4 * 6 + 4)
                all_max(S_M0, 7)

            stage_a(6, 0, True, {6: [m0_max]}, M_LATE)
            stage_a(7, 1, False, {2: [lambda: xob(0, 0)], 5: [lambda: qn_lo(0, 0)], 6: [lambda: qn_lo(0, 1)],
                                  8: [lambda: qn_lo(0, 2)], 9: [lambda: qn_lo(0, 3), lambda: xn_b(0, 0, xg[:, 1])]})
            for c in range(KC):
                h_lo_b(0, 0, c)

            def hid_lo(g, j):
                m, i = rows_of(j), j % 2
                pool.wait_ge(hid_hi_done, FC * g + j + 1)
                pool.tensor_tensor(hid[0:m, i, 1], hid_f[0:m, i], hid[0:m, i, 0], ALU.subtract).then_inc(hid_done, 1)

            def stage_b(g, par, more, load, extra={}):
                n, np = g + 1, 1 - par
                before = {1: [lambda: qn_lo(n, 0)], 2: [lambda: qn_lo(n, 1)], 3: [lambda: qn_lo(n, 2), lambda: xob(n, np)],
                          4: [lambda: qn_lo(n, 3)], 9: [lambda: h_lo_b(n, np, 1)], 10: [lambda: h_lo_b(n, np, 3)]}
                after = {6: [lambda: xn_b(n, np, xn2)], 8: [lambda: h_lo_b(n, np, 0)], 9: [lambda: h_lo_b(n, np, 2)]}
                for j in range(FC):
                    if more:
                        run(before, j)
                    hid_lo(g, j)
                    if more:
                        run(after, j)
                    run(extra, j)
                for t in range(TILES):
                    pool.wait_ge(y_read, 4 * g + t + 5)
                    pool.tensor_tensor(xg[:, par, t], xg[:, par, t], y_t[:, t % 2], ALU.add).then_inc(y_done, 1)


            def m1_max():
                pool.wait_ge(h2_done, 4 * 2 + 4 + 1)
                all_max(S_M1, 8)

            stage_b(0, 0, True, True)
            stage_b(1, 1, True, True, {8: [m1_max]})
            with pool.Fori(0, 2) as pair:
                for par in range(2):
                    stage_b(2 * pair + (2 + par), par, True, True)
            stage_b(6, 0, True, False)
            stage_b(7, 1, False, False)

        @block.scalar
        def _(act):
            primed(act, ((h_f_done, 4), (k_pos, 4), (q_read, 4), (z_read, 4), (h2_f_done, 4),
                         (silu_g_done, 1)))
            act.wait_ge(c_in, 16)
            act.activation(silu_c, ct, ACT.Silu).then_inc(silu_done, 1)

            def h_chunk(par, c, h_f_sem, scale, bias):
                act.activation(h[:, par, 0, c], bank[c % 2][:], ACT.Identity, bias=bias, scale=scale)
                act.activation(h_f[:, c % 2], bank[c % 2][:], ACT.Identity, bias=bias, scale=scale).then_inc(h_f_sem, 1)

            def h_a(n, par, c):
                b = n // PER_BATCH
                act.wait_ge(xT_done, 4 * n + c + 1)
                act.wait_ge(h_done, 4 * n + c + 3)
                if c == 0:
                    act.wait_ge(proj_done, OUTS * n + OUTS)
                h_chunk(par, c, h_f_done, modm[:, 0, c, bass.ds(b, 1)], modm[:, 1, c, bass.ds(b, 1)])

            def v_out(g, t):
                act.wait_ge(proj_done, OUTS * g + 2 * t + 2 + 2 * OUTS)
                act.wait_ge(kv_done, 4 * g + t + 3)
                act.activation(v_one[:, t % 2, :, 0:P],
                               bank[2 + (2 * t + 1) % 4][:].rearrange("p (k n) -> p k n", k=KC),
                               ACT.Copy, scale=c1(C_INV_V)).then_inc(v_read, 1)

            def k_out(g, t):
                act.wait_ge(proj_done, OUTS * g + 2 * t + 1 + 2 * OUTS)
                act.wait_ge(k_pos, 4 * g + t + 4)
                act.activation(k_t, bank[2 + 2 * t % 4][:], ACT.Copy, scale=c1(C_INV_K)).then_inc(k_read, 1)

            def k_acts(g, t):
                act.wait_ge(k_biased, 4 * g + t + 1)
                act.wait_ge(kp_done, 4 * g + t + 4)
                act.wait_ge(kv_done, 4 * g + t + 3)
                act.activation(k_e, k_t, ACT.Relu, scale=-1.0).then_inc(k_neg, 1)
                act.activation(kp[:, t % 2], k_t, ACT.Relu).then_inc(k_pos, 1)
                act.wait_ge(k_neg, 4 * g + t + 1)
                act.activation(k_e, k_e, ACT.Exp, scale=-1.0).then_inc(k_act, 1)

            def q_acts(g, c):
                act.wait_ge(proj_done, OUTS * g + 2 * TILES + c + 1 + 2 * OUTS)
                act.wait_ge(qp_done, 4 * g + c + 4)
                if c == 0:
                    act.wait_ge(qp_out, 16 * g + 16)
                src = bank[2 + c]
                act.activation(q_e, src[:], ACT.Relu, bias=qb_neg[:, c:c + 1], scale=c1(C_NEG_Q)).then_inc(q_neg, 1)
                act.activation(qp[:, c], src[:], ACT.Relu, bias=qb_col[:, c:c + 1], scale=c1(C_INV_Q)).then_inc(q_read, 1)
                act.wait_ge(q_neg, 4 * g + c + 1)
                act.activation(q_e, q_e, ACT.Exp, scale=-1.0).then_inc(q_act, 1)

            def stage_a(g, par, more, extra={}, late=0):
                for o in range(OUTS):
                    if o < 2 * TILES and o % 2 == 0:
                        k_out(g, o // 2)
                    if o < 2 * TILES and o % 2 == 1:
                        k_acts(g, o // 2)
                        v_out(g, o // 2)
                    if o >= 2 * TILES:
                        q_acts(g, o - 2 * TILES)
                    if more and 0 <= o - late - XT_SLOT < KC:
                        h_a(g + 1, 1 - par, o - late - XT_SLOT)
                    run(extra, o)

            def qs_all(n, q, s, count):
                act.wait_ge(s, count)
                for c in range(KC):
                    act.activation(q[:, c], q[:, c], ACT.Copy,
                                   scale=ksq[:, bass.ds(n // PER_BATCH, 1), c]).then_inc(qs_done, 1)

            def den(n, c):
                k = 4 * n + c + 1
                act.wait_ge(z_done, k)
                act.wait_ge(qn_done, k + 2)
                act.activation(qn_f[:, c % 2], bank[c % 2][:], ACT.Copy, bias=ATTN_EPS / SEQ).then_inc(z_read, 1)

            def qn_hi(n, c):
                act.wait_ge(qn_f_done, 4 * n + c + 1)
                if c == 0:
                    act.wait_ge(o_done, 4 * n + 4)
                act.activation(qn[:, 0, c], qn_f[:, c % 2], ACT.Copy).then_inc(qn_hi_done, 1)

            def h_b(n, par, c):
                b = n // PER_BATCH
                act.wait_ge(x2T_done, 4 * n + c + 5)
                act.wait_ge(h2_done, 4 * n + c + 3)
                if c == 0:
                    act.wait_ge(up_done, FC * n + FC)
                h_chunk(par, c, h2_f_done, modm[:, 2, c, bass.ds(b, 1)], modm[:, 3, c, bass.ds(b, 1)])

            def row_out(i):
                act.wait_ge(rows_done, i + 1)
                act.activation((ga_row, gb_row)[i // 2][:, i % 2], bank[ROW_BANK[i]][:], ACT.Copy).then_inc(rows_read, 1)

            act.wait_ge(nmr_done, 4)
            for t in range(TILES):
                act.activation(xg[:, 0, t], xg[:, 0, t], ACT.Identity, bias=nmr[:, t:t + 1],
                               scale=rstd[:, t:t + 1]).then_inc(xn_done, 1)
            act.wait_ge(h1_ready, 1)
            for c in range(KC):
                h_a(0, 0, c)
            row_out(0)
            row_out(1)
            stage_a(0, 0, True, {0: [lambda: act.wait_ge(v_ready, 1)], 2: [lambda: row_out(2)], 3: [lambda: row_out(3)],
                                 6: [lambda: act.wait_ge(q_ready, 1)]})
            with act.Fori(0, 2) as pair:
                for par in (1, 0):
                    stage_a(2 * pair + (2 - par), par, True)
            stage_a(5, 1, True)
            stage_a(6, 0, True, late=M_LATE)
            stage_a(7, 1, False, {1: [lambda: qs_all(0, q0, q0_in, 16)], 2: [lambda: den(0, 0), lambda: den(0, 1)],
                                  5: [lambda: qn_hi(0, 0), lambda: den(0, 2)],
                                  6: [lambda: qn_hi(0, 1), lambda: den(0, 3)], 7: [lambda: qn_hi(0, 2)],
                                  9: [lambda: qn_hi(0, 3)]})
            for c in range(KC):
                h_b(0, 0, c)

            def silu_gate(g, j):
                m = rows_of(j)
                act.wait_ge(gate_done, FC * g + j + 1)
                act.wait_ge(hid_f_done, FC * g + FC + last_use(j))
                act.activation(silu_g[0:m, j % 2], bank[6][0:m], ACT.Silu, scale=c1(C_INV_G)[0:m]).then_inc(silu_g_done, 1)

            def hid_hi(g, j):
                m, i = rows_of(j), j % 2
                act.wait_ge(hid_f_done, FC * g + j + 1 + FC)
                act.wait_ge(down_done, FC * g + FC + last_use(j))
                act.activation(hid[0:m, i, 0], hid_f[0:m, i], ACT.Copy).then_inc(hid_hi_done, 1)

            def stage_b(g, par, more, load):
                n, np = g + 1, 1 - par
                before = {0: [lambda: den(n, 0)], 1: [lambda: qn_hi(n, 0), lambda: den(n, 1)],
                          2: [lambda: qn_hi(n, 1), lambda: den(n, 2)], 3: [lambda: qn_hi(n, 2), lambda: den(n, 3)],
                          4: [lambda: qn_hi(n, 3)], 8: [lambda: h_b(n, np, 0)], 9: [lambda: h_b(n, np, 2)]}
                after = {8: [lambda: h_b(n, np, 1)], 9: [lambda: h_b(n, np, 3)]}
                for j in range(FC):
                    silu_gate(g, j)
                    if more:
                        run(before, j)
                    hid_hi(g, j)
                    if more:
                        run(after, j)
                    if load and j == FC - 4:
                        qs_all(n + 1, qp, q_in, 16 * (n + 1))

            qs_all(1, qp, q_in, 16)
            stage_b(0, 0, True, True)
            stage_b(1, 1, True, True)
            with act.Fori(0, 2) as pair:
                for par in range(2):
                    stage_b(2 * pair + (2 + par), par, True, True)
            stage_b(6, 0, True, False)
            stage_b(7, 1, False, False)

        @block.vector
        def _(dve):
            primed(dve, ((kv_read, 2), (look, STEPS), (hid_f_done, FC), (y_read, 4)))
            step = [0]

            def link(ins):
                step[0] += 1
                ins.then_inc(dve_step, 1)
                dve.wait_ge(dve_step, step[0])

            def pow2(n):
                link(dve.tensor_scalar(c1(C_TMP), c1(C_AMAX + n), 1e-30, None, ALU.max))
                bits = c1(C_TMP).bitcast(U32)
                link(dve.tensor_scalar(c1(C_POW + n).bitcast(U32), bits, EXPONENT, None, ALU.bitwise_and))
                link(dve.tensor_scalar(c1(C_INV + n).bitcast(U32), bits, EXPONENT, EXPONENT,
                                       ALU.bitwise_and, ALU.bitwise_xor))

            def absmax(src, n):
                axis = {1: AX.X, 2: AX.XY, 3: AX.XYZ}[len(src.shape) - 1]
                dve.tensor_reduce(c1(C_MAX + n), src, axis, ALU.max, apply_absolute_value=True).then_inc(maxed, 1)

            def weight(i, n, count, col):
                dve.wait_ge(reduced, count)
                pow2(n)
                link(dve.tensor_scalar(c1(C_SPLIT), c1(C_INV + n), 2.0 ** 13, None, ALU.mult))
                link(dve.tensor_scalar(flat(whi[:, i]), flat(raw[i]), c1(C_SPLIT), None, ALU.mult))
                dve.scalar_tensor_tensor(flat(wlo[:, i]), flat(raw[i]), c1(C_SPLIT), flat(whi[:, i]),
                                         ALU.mult, ALU.subtract).then_inc(w_split, 1)
                if n != S_K:
                    inverse(col, n)

            def inverse(col, n):
                link(dve.scalar_tensor_tensor(c1(col), c1(C_POW + S_H1), 2.0 ** -23, c1(C_POW + n), ALU.mult, ALU.mult))

            def mod_columns(s, n):
                src = bank[COL_BANK[s // 2]][:, 0:2 * KC * BATCHES].rearrange("p (s k b) -> p s k b", s=2, k=KC)
                dve.tensor_scalar(mods[:, s], src[:, 0], 1.0, None, ALU.add)
                link(dve.tensor_scalar(mods[:, s + 1], src[:, 1], 1.0, 0.0, ALU.mult, ALU.add))
                absmax(mods[:, s:s + 2], n)

            def mod_scale(s, n):
                pow2(n)
                link(dve.tensor_scalar(c1(C_SPLIT), c1(C_INV + n), 2.0 ** 8, None, ALU.mult))
                link(dve.tensor_scalar(modm[:, s:s + 2].rearrange("p a b c -> p (a b c)"),
                                       mods[:, s:s + 2].rearrange("p a b c -> p (a b c)"), c1(C_SPLIT), None, ALU.mult))

            def stats_a(n, par):
                dve.wait_ge(x_in[par], 16 * (n // 2 + 1))
                dve.wait_ge(nmr_done, 2 * n + 2)
                for t in range(TILES):
                    dve.bn_stats(stats[:, t], xg[:, par, t]).then_inc(stats_raw, 1)
                for t in range(TILES):
                    wait_apart(dve, stats_raw, 4 * n + t + 1)
                    dve.bn_aggr(mv[:, t], stats[:, t]).then_inc(stats_done, 1)

            dve.wait_ge(lut_in, 16)
            absmax(lut_f, S_LUT)
            for b in range(BATCHES):
                dve.memset(kv[:, b].rearrange("p k n -> p (k n)"), 0.0).then_inc(dve_step, 1)
                step[0] += 1
            dve.wait_ge(silu_done, 1)
            for b in range(BATCHES):
                for k in range(KC):
                    dve.tensor_copy(silu_cr[:, k, b], silu_c[:, k, b:b + 1].to_broadcast([P, P])).then_inc(rep_done, 1)
            dve.wait_ge(reduced, 1)
            pow2(S_LUT)
            link(dve.tensor_scalar(c1(C_SPLIT), c1(C_INV + S_LUT), 2.0 ** 13, None, ALU.mult))
            link(dve.tensor_scalar(lut_s, lut_f, c1(C_SPLIT), None, ALU.mult))
            link(dve.tensor_copy(tab_h[:, :, 0], lut_s))
            link(dve.tensor_tensor(tab_h[:, :, 1], lut_s, tab_h[:, :, 0], ALU.subtract))
            pairs = tab[:, :].rearrange("p (j b) -> p j b", b=2)
            link(dve.tensor_tensor(tab_x[:], pairs[:, :, 0], pairs[:, :, 1], ALU.bitwise_xor))
            stats_a(0, 0)
            dve.wait_ge(raw_in[0], 16)
            absmax(raw[0], S_K)
            weight(0, S_K, 2, C_INV_K)
            dve.wait_ge(cols_done, 1)
            mod_columns(0, S_H1)
            dve.wait_ge(reduced, 3)
            mod_scale(0, S_H1)
            inverse(C_INV_K, S_K)
            dve.sem_inc(h1_ready, 1)
            dve.wait_ge(raw_in[1], 16)
            absmax(raw[1], S_V)
            weight(1, S_V, 4, C_INV_V)
            dve.sem_inc(v_ready, 1)
            dve.wait_ge(raw_in[2], 16)
            absmax(raw[2], S_Q)
            weight(2, S_Q, 5, C_INV_Q)
            link(dve.tensor_scalar(c1(C_NEG_Q), c1(C_INV_Q), -1.0, None, ALU.mult))
            dve.wait_ge(rows_in, 5 * 16)
            link(dve.tensor_scalar(qb_neg[:], qb_col[:], -1.0, None, ALU.mult))
            dve.sem_inc(q_ready, 1)

            def h2_columns():
                dve.wait_ge(cols_done, 2)
                mod_columns(2, S_H2)

            def h2_scales():
                dve.wait_ge(reduced, 6)
                mod_scale(2, S_H2)
                e_l, e_h, r_l, r_h = c1(C_POW + S_LUT), c1(C_POW + S_H2), c1(C_INV + S_LUT), c1(C_INV + S_H2)
                link(dve.scalar_tensor_tensor(c1(C_INV_G), e_l, 2.0 ** -23, e_h, ALU.mult, ALU.mult))
                link(dve.scalar_tensor_tensor(c1(C_HID), r_l, 2.0 ** -34, r_h, ALU.mult, ALU.mult))
                link(dve.tensor_tensor(c1(C_TMP), e_l, e_h, ALU.mult))
                link(dve.tensor_tensor(c1(C_TMP + 1), c1(C_TMP), c1(C_TMP), ALU.mult))
                link(dve.scalar_tensor_tensor(c1(C_INV_D), c1(C_TMP + 1), 2.0 ** -5, e_l, ALU.mult, ALU.mult))

            def clamp(row, temps):
                sign, size = (temps[:, i].bitcast(U32) for i in range(2))
                link(dve.tensor_scalar(sign.bitcast(F32), row, 0.0, None, ALU.is_ge))
                link(dve.tensor_scalar(size, row.bitcast(U32), MAGNITUDE, None, ALU.bitwise_and))
                link(dve.tensor_scalar(sign.bitcast(F32), sign.bitcast(F32), 2.0, -1.0, ALU.mult, ALU.add))
                link(dve.scalar_tensor_tensor(row, size.bitcast(F32), 0.25, sign.bitcast(F32), ALU.max, ALU.mult))

            def look_step(p, wide, i, done):
                kind, dst, a, b, need = LOOK_STEPS[i]
                words = w_ffn[:, bass.ds(p * GROUP, GROUP * (2 if wide else 1))]

                def buf(k):
                    k = LOOK_BUFS.index(k)
                    return look_wide[k] if wide else look_buf[:, k]

                if done + need:
                    dve.wait_ge(look, done + need)
                if kind == "bit":
                    ins = dve.tensor_scalar(buf(dst), words, a, None, ALU.bitwise_and)
                elif kind == "ones":
                    ins = dve.tensor_scalar(buf(dst).bitcast(I32), words.bitcast(I32), 31, 31,
                                            ALU.logical_shift_left, ALU.arith_shift_right)
                elif kind == "leaf":
                    ins = dve.tensor_scalar(buf(dst), buf("m0"), tab_x[:, a:a + 1], tab[:, 2 * a:2 * a + 1],
                                            ALU.bitwise_and, ALU.bitwise_xor)
                elif kind == "store":
                    ins = dve.tensor_copy(words, buf(a))
                else:
                    ins = dve.copy_predicated(buf(dst), buf(a), buf(b))
                ins.then_inc(look, 1)

            def in_twos(first, pieces):
                return [(first + p, p + 1 < pieces) for p in range(0, pieces, 2)]

            def lookup(units, before, share, shares):
                total = len(units) * STEPS
                if share == 0:
                    dve.wait_ge(look, before)
                    dve.sem_clear(look)
                for i in range(total * share // shares, total * (share + 1) // shares):
                    p, wide = units[i // STEPS]
                    look_step(p, wide, i % STEPS, i // STEPS * STEPS)

            def kv_sum(g):
                dve.wait_ge(kv_done, 4 * g + 8)
                for i in range(2):
                    acc = kv[:, g // PER_BATCH, 2 * i:2 * i + 2]
                    dve.wait_ge(kv_read, 2 * g + i + 1)
                    dve.tensor_tensor(acc, acc, kv_bank[i], ALU.add).then_inc(kv_read, 1)

            def stage_a(g, par, more, look=None, extra={}):
                if more:
                    stats_a(g + 1, 1 - par)
                for o in range(OUTS):
                    run(extra, o)
                    if o == OUTS - 2:
                        kv_sum(g)
                    if look:
                        units, before, share, shares = look
                        lookup(units, before, share + o, shares)

            def m_att(b):
                link(dve.tensor_scalar(ksq[:, b], kv[:, b, :, P], 1.0 / SEQ, None, ALU.mult))
                link(dve.tensor_scalar(krec[:], kv[:, b, :, P], 1e-30, None, ALU.max))
                link(dve.reciprocal(krec[:], krec[:]))
                for c in range(KC):
                    a = kv[:, b, c, 0:P]
                    link(dve.scalar_tensor_tensor(a, a, krec[:, c:c + 1], vb_row[:, c * P:(c + 1) * P], ALU.mult, ALU.add))
                    link(dve.tensor_tensor(a, a, same_head[:], ALU.mult))
                dve.sem_inc(att_done, 1)

            def m_attT(b):
                dve.wait_ge(attT_done, b + 1)
                dve.tensor_copy(att_T[b], bank[0][:].rearrange("p (k n) -> p k n", k=KC)).then_inc(attT_read, 1)

            def m_out(b, c):
                dve.wait_ge(m_done, b * KC + c + 1)
                dve.tensor_tensor(m_full[:, b * KC + c], bank[(c + 1) % 2][:], ga_row[:, b], ALU.mult).then_inc(m_read, 1)

            def m_max(b):
                dve.wait_ge(m_read, b * KC + KC)
                absmax(m_full[:, b * KC:b * KC + KC], S_M0 + b)

            def m_scale(b):
                dve.wait_ge(reduced, 7 + b)
                pow2(S_M0 + b)
                link(dve.tensor_scalar(c1(C_SPLIT), c1(C_INV + S_M0 + b), 2.0 ** 13, None, ALU.mult))
                link(dve.tensor_scalar(c1(C_INV_O + b), c1(C_POW + S_M0 + b), 2.0 ** -29, None, ALU.mult))

            def m_cut(b, c):
                c = b * KC + c
                link(dve.tensor_scalar(m_tmp[b], m_full[:, c], c1(C_SPLIT), None, ALU.mult))
                link(dve.tensor_copy(m_split[:, c, 0], m_tmp[b]))
                link(dve.tensor_tensor(m_split[:, c, 1], m_tmp[b], m_split[:, c, 0], ALU.subtract))

            def o_bias(b):
                link(dve.tensor_tensor(obga[:, b], obga[:, b], ga_row[:, b], ALU.mult))
                dve.sem_inc(obga_ready, 1)

            def qn_full(n, q, c):
                k = 4 * n + c + 1
                dve.wait_ge(z_read, k + 4)
                dve.reciprocal(qn_f[:, c % 2], qn_f[:, c % 2]).then_inc(rec_done, 1)
                dve.wait_ge(rec_done, k)
                dve.scalar_tensor_tensor(qn_f[:, c % 2], q[:, c], 2.0 ** 15, qn_f[:, c % 2],
                                         ALU.mult, ALU.mult).then_inc(qn_f_done, 1)

            def x1_tile(n, par, t):
                k = 4 * n + t + 1
                dve.wait_ge(o_done, k + 4)
                dve.wait_ge(xob_done, k)
                dve.scalar_tensor_tensor(xg[:, par, t], bank[t % 2][:], c1(C_INV_O + n // PER_BATCH), xg[:, par, t],
                                         ALU.mult, ALU.add).then_inc(x1_done, 1)
                dve.wait_ge(x1_done, k)
                if t == 0:
                    dve.wait_ge(nmr2_done, 2 * n + 2)
                dve.bn_stats(stats[:, t], xg[:, par, t]).then_inc(stats2_raw, 1)
                wait_apart(dve, stats2_raw, k)
                dve.bn_aggr(mv[:, t], stats[:, t]).then_inc(stats2_done, 1)

            dve.wait_ge(idx_first, 6 * 16)
            pair_steps = -(-LOOK_PAIR // 2) * STEPS
            stage_a(0, 0, True, (in_twos(0, LOOK_0), STEPS, 0, OUTS), {3: [h2_columns], 5: [h2_scales]})
            steps_0 = -(-LOOK_0 // 2) * STEPS
            dve.wait_ge(look, steps_0)
            dve.sem_inc(look, pair_steps - steps_0)
            dve.wait_ge(idx_rest, (FC - 2) * 3 * 16)
            with dve.Fori(0, 2) as pair:
                units = in_twos(LOOK_PAIR * pair + LOOK_0, LOOK_PAIR)
                for par in (1, 0):
                    stage_a(2 * pair + (2 - par), par, True, (units, pair_steps, (1 - par) * OUTS, 2 * OUTS))
            dve.wait_ge(rows_read, 4)
            stage_a(5, 1, True, (in_twos(LOOK_0 + 2 * LOOK_PAIR, LOOK_5), pair_steps, 0, OUTS),
                    {0: [lambda: clamp(ga_row[:, 0], hid_f)], 6: [lambda: m_att(0)], 11: [lambda: m_attT(0)]})
            dve.wait_ge(look, LOOK_5 // 2 * STEPS)
            dve.sem_inc(looked, 1)
            first_6 = LOOK_A - LOOK_7 - LOOK_6
            stage_a(6, 0, True, ([(first_6 + p, False) for p in range(LOOK_6)], LOOK_5 // 2 * STEPS, 0, OUTS),
                    {3: [lambda: m_out(0, 0), lambda: m_out(0, 1)],
                     4: [lambda: m_out(0, 2), lambda: m_out(0, 3)], 5: [lambda: m_max(0)], 6: [lambda: o_bias(0)],
                     8: [lambda: m_scale(0)], 9: [lambda: m_cut(0, 0)], 10: [lambda: m_cut(0, 1)], 11: [lambda: m_cut(0, 2)]})

            def look_7(*shares):
                for share in shares:
                    lookup([(first_6 + LOOK_6 + p, False) for p in range(LOOK_7)], LOOK_6 * STEPS, share, OUTS)

            stage_a(7, 1, False, extra={
                0: [lambda: m_cut(0, 3), lambda: look_7(0, 1), lambda: dve.sem_inc(m_ready, 1)], 1: [lambda: look_7(2, 3)],
                2: [lambda: qn_full(0, q0, 0)], 4: [lambda: qn_full(0, q0, 1)], 6: [lambda: qn_full(0, q0, 2)],
                8: [lambda: qn_full(0, q0, 3), lambda: look_7(4, 5)],
                9: [lambda: x1_tile(0, 0, 0), lambda: look_7(6), lambda: x1_tile(0, 0, 1), lambda: look_7(7),
                    lambda: x1_tile(0, 0, 2), lambda: x1_tile(0, 0, 3)]})
            look_7(8, 9, 10)

            def hid_full(g, j):
                m, i = rows_of(j), j % 2
                k = FC * g + j + 1
                dve.wait_ge(silu_g_done, k + 1)
                dve.wait_ge(up_done, k + 2 * FC)
                dve.wait_ge(hid_done, FC * g + FC + last_use(j))
                dve.scalar_tensor_tensor(hid_f[0:m, i], bank[7][0:m], c1(C_HID)[0:m], silu_g[0:m, i],
                                         ALU.mult, ALU.mult).then_inc(hid_f_done, 1)

            def y_tile(g, t):
                k = 4 * g + t + 1
                dve.wait_ge(y_done, k + 2)
                dve.scalar_tensor_tensor(y_t[:, t % 2], bank[2 + t][:], c1(C_INV_D), gb_row[:, g // PER_BATCH],
                                         ALU.mult, ALU.mult).then_inc(y_read, 1)

            def look_b(share):
                lookup([(PIECES - LOOK_B0 + p, False) for p in range(LOOK_B0)], LOOK_7 * STEPS, share, FC - 3)

            def stage_b(g, par, more, load, looks=False, extra={}, early={}):
                n, np = g + 1, 1 - par
                before = {5: [lambda: x1_tile(n, np, 1)], 6: [lambda: x1_tile(n, np, 3)]}
                after = {0: [lambda: qn_full(n, qp, 0)], 1: [lambda: qn_full(n, qp, 1)], 2: [lambda: qn_full(n, qp, 2)],
                         3: [lambda: qn_full(n, qp, 3)], 4: [lambda: x1_tile(n, np, 0)], 5: [lambda: x1_tile(n, np, 2)]}
                for j in range(FC):
                    if more:
                        run(before, j)
                    run(early, j)
                    hid_full(g, j)
                    if more:
                        run(after, j)
                    run(extra, j)
                    if looks and j < FC - 2:
                        if j:
                            look_b(j - 1)
                        else:
                            look_7(11)
                            dve.wait_ge(look, LOOK_7 * STEPS)
                            dve.sem_inc(looked, 1)
                        if j == 5:
                            dve.wait_ge(look, (LOOK_B0 - PARTS) * STEPS)
                            dve.sem_inc(looked, 1)
                        if j == FC - 3:
                            dve.wait_ge(look, LOOK_B0 * STEPS)
                            dve.sem_inc(looked, 1)
                if more:
                    dve.wait_ge(down_done, FC * g + 2 * FC)
                for t in range(TILES):
                    if not more:
                        dve.wait_ge(last_sum, t + 1)
                    y_tile(g, t)

            stage_b(0, 0, True, True, True, {
                6: [lambda: clamp(ga_row[:, 1], y_t), lambda: o_bias(1)], 7: [lambda: clamp(gb_row[:, 0], y_t)],
                8: [lambda: clamp(gb_row[:, 1], y_t)]})
            stage_b(1, 1, True, True, extra={
                2: [lambda: m_att(1)], 6: [lambda: m_attT(1)], 7: [lambda: m_out(1, 2), lambda: m_out(1, 3), lambda: m_max(1)],
                8: [lambda: m_scale(1)], 9: [lambda: m_cut(1, 0), lambda: m_cut(1, 1)],
                10: [lambda: m_cut(1, 2), lambda: m_cut(1, 3), lambda: dve.sem_inc(m_ready, 1)]},
                early={7: [lambda: m_out(1, 0), lambda: m_out(1, 1)]})
            with dve.Fori(0, 2) as pair:
                for par in range(2):
                    stage_b(2 * pair + (2 + par), par, True, True)
            stage_b(6, 0, True, False)
            stage_b(7, 1, False, False)

        @block.tensor
        def _(pe):
            primed(pe, ((proj_done, 2 * OUTS), (kv_done, 4), (o_done, 4), (x2T_done, 4), (up_done, 2 * FC), (down_done, FC)))

            def three(dst, pairs, start=True, stop=True):
                last = None
                for i, ((a_hi, a_lo), (b_hi, b_lo)) in enumerate(pairs):
                    first, end = start and i == 0, stop and i == len(pairs) - 1
                    pe.matmul(dst, a_hi, b_hi, start=first, stop=False)
                    pe.matmul(dst, a_hi, b_lo, start=False, stop=False)
                    last = pe.matmul(dst, a_lo, b_hi, start=False, stop=end)
                return last

            def turn(src, c, done):
                for t in range(TILES):
                    last = pe.transpose(bank[c % 2][:, t * P:(t + 1) * P], src[:, t, c * P:(c + 1) * P], ident[:])
                last.then_inc(done, 1)

            def xT_a(n, par, c):
                if c == 0:
                    pe.wait_ge(xn_done, 4 * n + 4)
                pe.wait_ge(h_f_done, 4 * n + c + 3)
                turn(xg[:, par], c, xT_done)

            def out_a(g, par, o):
                if o == 0:
                    pe.wait_ge(h_done, 4 * g + 8)
                if o < 4:
                    pe.wait_ge(q_read, 4 * g + o + 1)
                elif o % 2 == 0:
                    pe.wait_ge(k_read, 4 * g + (o - 4) // 2 + 1)
                else:
                    pe.wait_ge(v_read, 4 * g + (o - 5) // 2 + 1)
                h_chunks = [(h[:, par, 0, k], h[:, par, 1, k]) for k in range(KC)]
                if o < 2 * TILES:
                    t, w = o // 2, o % 2
                    pairs = [((hi[:, t * P:(t + 1) * P], lo[:, t * P:(t + 1) * P]), (whi[:, w, k], wlo[:, w, k]))
                             for k, (hi, lo) in enumerate(h_chunks)]
                else:
                    c = o - 2 * TILES
                    pairs = [((whi[:, 2, k, c * P:(c + 1) * P], wlo[:, 2, k, c * P:(c + 1) * P]), (hi, lo))
                             for k, (hi, lo) in enumerate(h_chunks)]
                three(bank[2 + o % 4][:], pairs).then_inc(proj_done, 1)

            def kv_a(g, t):
                pe.wait_ge(kp_done, 4 * g + t + 5)
                pe.wait_ge(v_read, 4 * g + t + 1)
                if t == 0:
                    pe.wait_ge(kv_read, 2 * g + 2)
                for c in range(KC):
                    n = P + 1
                    at = (c % 2) * n
                    last = pe.matmul(bank[6 + c // 2][:, at:at + n], kp[:, t % 2, c * P:(c + 1) * P], v_one[:, t % 2, c],
                                     start=(t == 0 and c % 2 == 0), stop=(t == TILES - 1), skip_group_check=True)
                last.then_inc(kv_done, 1)

            def stage_a(g, par, more, extra={}, late=0, first=False):
                for o in range(OUTS):
                    if first and o in (0, 1, 2 * TILES):
                        pe.wait_ge(w_split, min(o + 1, 3))
                    out_a(g, par, o)
                    if first and o == 3:
                        pe.wait_ge(maxed, 3)
                    if o in (3, 5, 7, 9):
                        kv_a(g, (o - 3) // 2)
                    if more and 0 <= o - late - XT_SLOT < KC:
                        xT_a(g + 1, 1 - par, o - late - XT_SLOT)
                    run(extra, o)

            def m_turn(b):
                pe.wait_ge(att_done, b + 1)
                if b == 0:
                    pe.wait_ge(h_f_done, 4 * 6 + 3 + 4)
                else:
                    pe.wait_ge(x1_done, 4 * 2 + 3)
                for c in range(KC):
                    last = pe.transpose(bank[0][:, c * P:(c + 1) * P], kv[:, b, c, 0:P], ident[:])
                last.then_inc(attT_done, 1)

            def m_prod(b, c):
                if c == 0:
                    pe.wait_ge(ow_in[b], 16)
                    pe.wait_ge(attT_read, b + 1)
                    if b == 0:
                        pe.wait_ge(h_f_done, 4 * 6 + 4 + 4)
                    else:
                        pe.wait_ge(x1_done, 4 * 2 + 4)
                elif c > 1:
                    pe.wait_ge(m_read, b * KC + c - 1)
                pe.matmul(bank[(c + 1) % 2][:], att_T[b][:, c], owt[b][:, c], start=True, stop=True).then_inc(m_done, 1)

            def z_piece(n, q, c):
                pe.wait_ge(qs_done, 4 * n + c + 1)
                if c < 2:
                    pe.wait_ge(h2_f_done, 4 * n + c + 3)
                else:
                    pe.wait_ge(z_read, 4 * n + c + 3)
                pe.matmul(bank[c % 2][:], same_head[:], q[:, c], start=True, stop=True).then_inc(z_done, 1)

            def o_piece(n, t):
                b = n // PER_BATCH
                if t == 0:
                    pe.wait_ge(m_ready, b + 1)
                    pe.wait_ge(qn_done, 4 * n + 8)
                if t < 2:
                    pe.wait_ge(z_read, 4 * n + 3 + t + 4)
                else:
                    pe.wait_ge(x1_done, 4 * n + t - 1)
                pairs = [((qn[:, 0, c, t * P:(t + 1) * P], qn[:, 1, c, t * P:(t + 1) * P]),
                          (m_split[:, b * KC + c, 0], m_split[:, b * KC + c, 1])) for c in range(KC)]
                three(bank[t % 2][:], pairs).then_inc(o_done, 1)

            def t_piece(n, rows, c):
                if c == 0:
                    pe.wait_ge(xn2_done, 4 * n + 4)
                if c < 2:
                    pe.wait_ge(x1_done, 4 * n + 3 + c)
                else:
                    pe.wait_ge(h2_f_done, 4 * n + c + 3)
                turn(rows, c, x2T_done)

            def columns(slot, s):
                pe.wait_ge(mod_in[s], 16)
                for c in range(KC):
                    at = (slot % 2 * KC + c) * BATCHES
                    for k in range(KC):
                        last = pe.matmul(bank[COL_BANK[slot // 2]][:, at:at + BATCHES], mod_raw[s][:, k, c * P:(c + 1) * P], silu_c[:, k],
                                         start=(k == 0), stop=(k == KC - 1), skip_group_check=True)
                if slot % 2:
                    last.then_inc(cols_done, 1)

            def row(i, s):
                pe.wait_ge(mod_in[s], 16)
                for k in range(KC):
                    last = pe.matmul(bank[ROW_BANK[i]][:], silu_cr[:, k, i % 2], mod_raw[s][:, k],
                                     start=(k == 0), stop=(k == KC - 1))
                last.then_inc(rows_done, 1)

            pe.wait_ge(silu_done, 1)
            columns(0, 1)
            columns(1, 0)
            pe.wait_ge(pool_step, 3 + P // HEAD)
            xT_a(0, 0, 0)
            xT_a(0, 0, 1)
            pe.wait_ge(rep_done, BATCHES * KC)
            row(0, 2)
            xT_a(0, 0, 2)
            xT_a(0, 0, 3)
            row(1, 2)

            def row_b(b):
                pe.wait_ge(h_f_done, 4 + 3 + b)
                row(2 + b, 5)

            def columns_b():
                pe.wait_ge(rows_read, 3)
                columns(2, 4)

            stage_a(0, 0, True, {0: [lambda: row_b(0)], 1: [lambda: row_b(1), lambda: pe.wait_ge(rows_read, 2)], 2: [columns_b], 3: [lambda: columns(3, 3)],
                                 4: [lambda: pe.wait_ge(maxed, 6), lambda: pe.wait_ge(rows_read, 4)]}, first=True)
            with pe.Fori(0, 2) as pair:
                for par in (1, 0):
                    stage_a(2 * pair + (2 - par), par, True)
            stage_a(5, 1, True, {10: [lambda: m_turn(0)]})
            stage_a(6, 0, True, {3: [lambda: m_prod(0, 0), lambda: m_prod(0, 1)],
                                 4: [lambda: m_prod(0, 2), lambda: m_prod(0, 3)], 5: [lambda: pe.wait_ge(m_read, KC)]}, M_LATE)
            stage_a(7, 1, False, {0: [lambda: pe.wait_ge(h_f_done, 4 * 8 + 4)],
                                  2: [lambda: z_piece(0, q0, 0), lambda: z_piece(0, q0, 1)],
                                  4: [lambda: z_piece(0, q0, 2)], 6: [lambda: z_piece(0, q0, 3)],
                                  9: [lambda t=t: o_piece(0, t) for t in range(TILES)]})
            for c in range(KC):
                t_piece(0, xg[:, 1], c)

            def gate_up(g, par, j, w, dst):
                m = rows_of(j)
                pairs = [((ffn[:, j, w, k, 0:m, 0], ffn[:, j, w, k, 0:m, 1]), (h[:, par, 0, k], h[:, par, 1, k]))
                         for k in range(KC)]
                return three(dst[0:m], pairs)

            def gate(g, par, j):
                if j == 0:
                    pe.wait_ge(h2_done, 4 * g + 8)
                pe.wait_ge(silu_g_done, FC * g + j + 1)
                gate_up(g, par, j, 0, bank[6]).then_inc(gate_done, 1)

            def up(g, par, j):
                pe.wait_ge(hid_f_done, FC * g + FC + j)
                gate_up(g, par, j, 1, bank[7]).then_inc(up_done, 1)

            def down(g, j, tilewise=False):
                m, i = rows_of(j), j % 2
                pe.wait_ge(hid_done, FC * g + j + 1 + FC)
                if j == 0:
                    pe.wait_ge(y_read, 4 * g + 4)
                w_down = ffn[:, j, 2].rearrange("p k n h -> p (k n) h")
                for t in range(TILES):
                    pairs = [((hid[0:m, i, 0, t * P:(t + 1) * P], hid[0:m, i, 1, t * P:(t + 1) * P]),
                              (w_down[0:m, :, 0], w_down[0:m, :, 1]))]
                    last = three(bank[2 + t][:], pairs, start=(j == 0), stop=(j == FC - 1))
                    if tilewise:
                        last.then_inc(last_sum, 1)
                if not tilewise:
                    last.then_inc(down_done, 1)

            def stage_b(g, par, more, before={}, after={}, looks=False):
                n, np = g + 1, 1 - par
                b_attn = {0: [lambda: z_piece(n, qp, 0)], 1: [lambda: z_piece(n, qp, 1)], 2: [lambda: z_piece(n, qp, 2)],
                          3: [lambda: z_piece(n, qp, 3)], 5: [lambda: o_piece(n, 1)], 6: [lambda: o_piece(n, 3)],
                          8: [lambda: t_piece(n, xn2, 0)], 9: [lambda: t_piece(n, xn2, 2)]}
                a_attn = {4: [lambda: o_piece(n, 0)], 5: [lambda: o_piece(n, 2)], 8: [lambda: t_piece(n, xn2, 1)],
                          9: [lambda: t_piece(n, xn2, 3)]}
                for j in range(FC):
                    if looks and j >= FC - 3:
                        pe.wait_ge(looked, j - (FC - 3) + 2)
                    if j:
                        gate(g, par, j)
                    run(before, j)
                    if more:
                        run(b_attn, j)
                    up(g, par, j)
                    if j:
                        down(g, j - 1)
                    if more:
                        run(a_attn, j)
                    run(after, j)
                if more:
                    gate(g + 1, np, 0)
                down(g, FC - 1, tilewise=not more)

            pe.wait_ge(m_ready, 1)
            pe.wait_ge(kv_read, 2 * GROUPS + 2)
            pe.wait_ge(q_read, 4 * GROUPS + 4)
            gate(0, 0, 0)
            stage_b(0, 0, True, looks=True)
            stage_b(1, 1, True,
                    {7: [lambda: m_prod(1, 0), lambda: m_prod(1, 1)], 8: [lambda: pe.wait_ge(m_read, 2 * KC)]},
                    {6: [lambda: m_turn(1)], 7: [lambda: m_prod(1, 2), lambda: m_prod(1, 3)]})
            with pe.Fori(0, 2) as pair:
                for par in range(2):
                    stage_b(2 * pair + (2 + par), par, True)
            stage_b(6, 0, True)
            stage_b(7, 1, False)


_INS = ["x", "qwT", "qb", "kwT", "kb", "vwT", "vb", "owT", "ob", "lut", "gateT", "upT", "downT", "cT", "wmod"]


def kernel(**inputs):
    import numpy as np
    import concourse.bacc as bacc
    from concourse import mybir as _mybir
    from concourse.bass_utils import run_bass_kernel_spmd

    def t(name):
        return np.ascontiguousarray(np.asarray(inputs[name]).T)

    def a(name):
        return np.ascontiguousarray(np.asarray(inputs[name]))

    laid = dict(
        x=a("L0_attn_hidden_states"),
        qwT=t("L0_attn_q_w"), qb=np.ascontiguousarray(a("L0_attn_q_b").reshape(KC, P).T), kwT=t("L0_attn_k_w"), kb=a("L0_attn_k_b"),
        vwT=t("L0_attn_v_w"), vb=a("L0_attn_v_b"), owT=t("L0_attn_o_w"), ob=a("L0_attn_o_b"),
        lut=a("L0_ffn_lut"), gateT=t("L0_ffn_gate_idx"), upT=t("L0_ffn_up_idx"), downT=t("L0_ffn_down_idx"),
        cT=t("L0_c"), wmod=a("L0_wmod"),
    )
    nc = bacc.Bacc("TRN2", target_bir_lowering=False, num_devices=1)
    arrays, args = {}, []
    for name in _INS:
        arrays[f"in_{name}"] = laid[name]
        args.append(nc.dram_tensor(f"in_{name}", laid[name].shape, _mybir.dt.from_np(laid[name].dtype),
                                   kind="ExternalInput").ap())
    args.append(nc.dram_tensor("out_0", laid["x"].shape, _mybir.dt.float32, kind="ExternalOutput").ap())
    adaln_kernel(nc, *args)
    r = run_bass_kernel_spmd(nc, [arrays], core_ids=[0])
    return r.results[0]["out_0"]
```
